# Optimizing a Trainium2 kernel written in Bass

```python
import numpy as np
import jax
import jax.numpy as jnp

def _softmax(x, axis=-1):
    return jax.nn.softmax(x, axis=axis)

def _gelu(x):
    return jax.nn.gelu(x, approximate=True)

def _silu(x):
    return jax.nn.silu(x)

def _sigmoid(x):
    return jax.nn.sigmoid(x)

def _layernorm(x, axis=-1, eps=1e-05):
    m = jnp.mean(x, axis=axis, keepdims=True)
    v = jnp.var(x, axis=axis, keepdims=True)
    return (x - m) / jnp.sqrt(v + eps)

def _scatter_add(tgt, idx, src, axis=0):
    return tgt.at[idx].add(src)

def _segment_sum(src, seg, n):
    return jax.ops.segment_sum(src, seg, n)
kernel_name = 'mk_macaron_d1_jaxref_r4_ecbefa'

def setup_inputs(seed: int=0):
    np.random.seed(seed)
    _w = jnp.asarray

    def _L0_attn_setup():
        import jax, jax.numpy as jnp
        import numpy as np
        EPS = 1.1920929e-07

        def _rms(x):
            return x * jax.lax.rsqrt(jnp.mean(x * x, axis=-1, keepdims=True) + EPS)
        key = jax.random.key(seed)
        k0, k1, k2, k3 = jax.random.split(key, 4)
        B, S, D, DFF = (4, 512, 512, 2048)
        x = jax.random.normal(k0, (B, S, D), dtype=jnp.float32)
        w_qkv = jax.random.normal(k1, (3 * D, D), dtype=jnp.float32) * 0.02
        w_swiglu = jax.random.normal(k2, (2 * DFF, D), dtype=jnp.float32) * 0.02
        w_out = jax.random.normal(k3, (D, DFF), dtype=jnp.float32) * 0.02
        return {'x': x, 'w_qkv': w_qkv, 'w_swiglu': w_swiglu, 'w_out': w_out}
    _L0_attn_in = _L0_attn_setup()

    def _L0_ffn_setup():
        import jax, jax.numpy as jnp
        import numpy as np
        K = 2
        SCALING = 16.0 / 16.0
        key = jax.random.key(seed)
        ks = jax.random.split(key, 7)
        B, T, D, O, E, R = (2, 1024, 512, 512, 8, 16)
        return {'x': jax.random.normal(ks[0], (B, T, D), dtype=jnp.float32), 'W': jax.random.normal(ks[1], (O, D), dtype=jnp.float32) * (1.0 / np.sqrt(D)), 'b': jax.random.normal(ks[2], (O,), dtype=jnp.float32) * 0.02, 'lora_A': jax.random.normal(ks[3], (E, R, D), dtype=jnp.float32) * (1.0 / np.sqrt(D)), 'lora_B': jax.random.normal(ks[4], (E, O, R), dtype=jnp.float32) * 0.02, 'gate_w': jax.random.normal(ks[5], (E, D), dtype=jnp.float32) * 0.02, 'gate_b': jax.random.normal(ks[6], (E,), dtype=jnp.float32) * 0.02}
    _L0_ffn_in = _L0_ffn_setup()
    _d = {'L0_attn_x': _L0_attn_in['x'], 'L0_attn_w_qkv': _L0_attn_in['w_qkv'], 'L0_attn_w_swiglu': _L0_attn_in['w_swiglu'], 'L0_attn_w_out': _L0_attn_in['w_out'], 'L0_ffn_W': _L0_ffn_in['W'], 'L0_ffn_b': _L0_ffn_in['b'], 'L0_ffn_lora_A': _L0_ffn_in['lora_A'], 'L0_ffn_lora_B': _L0_ffn_in['lora_B'], 'L0_ffn_gate_w': _L0_ffn_in['gate_w'], 'L0_ffn_gate_b': _L0_ffn_in['gate_b']}
    _x0 = _d['L0_attn_x']
    _d['L0_attn_x'] = jax.random.normal(jax.random.fold_in(jax.random.key(seed), 1), (4, 1024, 512), dtype=_x0.dtype)
    del _x0
    return _d

def reference(L0_attn_x, L0_attn_w_qkv, L0_attn_w_swiglu, L0_attn_w_out, L0_ffn_W, L0_ffn_b, L0_ffn_lora_A, L0_ffn_lora_B, L0_ffn_gate_w, L0_ffn_gate_b):

    def _L0_attn_ref(x, w_qkv, w_swiglu, w_out):
        import jax, jax.numpy as jnp
        import numpy as np
        EPS = 1.1920929e-07

        def _rms(x):
            return x * jax.lax.rsqrt(jnp.mean(x * x, axis=-1, keepdims=True) + EPS)
        qkv = _rms(x) @ w_qkv.T
        q, k, v = jnp.split(qkv, 3, axis=-1)
        q = _rms(q)
        k = _rms(k)
        w = jnp.exp(k)
        kv_cum = jnp.cumsum(w * v, axis=1)
        w_cum = jnp.cumsum(w, axis=1)
        y = jax.nn.sigmoid(q) * (kv_cum / (w_cum + 1e-06))
        uv = y @ w_swiglu.T
        u, g = jnp.split(uv, 2, axis=-1)
        return x + u * jax.nn.silu(g) @ w_out.T

    def _L0_ffn_ref(x, W, b, lora_A, lora_B, gate_w, gate_b):
        import jax, jax.numpy as jnp
        import numpy as np
        K = 2
        SCALING = 16.0 / 16.0
        orig_shape = x.shape
        D = orig_shape[-1]
        O = W.shape[0]
        x_flat = x.reshape(-1, D)
        base = x_flat @ W.T + b
        logits = x_flat @ gate_w.T + gate_b
        topk_logits, topk_idx = jax.lax.top_k(logits, K)
        gates = jax.nn.softmax(topk_logits, axis=-1)
        xA = jnp.einsum('nd,erd->ner', x_flat, lora_A)
        delta_all = jnp.einsum('ner,eor->neo', xA, lora_B)
        delta_topk = jnp.take_along_axis(delta_all, topk_idx[:, :, None], axis=1)
        lora_update = jnp.sum(delta_topk * gates[:, :, None], axis=1)
        out = base + SCALING * lora_update
        return out.reshape(*orig_shape[:-1], O)
    x = L0_attn_x
    x = x + 0.5 * _L0_ffn_ref(_layernorm(x, axis=-1), L0_ffn_W, L0_ffn_b, L0_ffn_lora_A, L0_ffn_lora_B, L0_ffn_gate_w, L0_ffn_gate_b)
    x = x + _L0_attn_ref(_layernorm(x, axis=-1), L0_attn_w_qkv, L0_attn_w_swiglu, L0_attn_w_out)
    x = x + 0.5 * _L0_ffn_ref(_layernorm(x, axis=-1), L0_ffn_W, L0_ffn_b, L0_ffn_lora_A, L0_ffn_lora_B, L0_ffn_gate_w, L0_ffn_gate_b)
    return x

_drawn_inputs = setup_inputs


def setup_inputs(seed=0):
    import zlib

    import numpy as np

    out = dict(_drawn_inputs(seed))
    spreads = {}
    factors = {'L0_attn_w_qkv': 8.0,
     'L0_attn_w_swiglu': 8.0,
     'L0_attn_w_out': 8.0,
     'L0_ffn_b': 4.645,
     'L0_ffn_gate_b': 23.551}
    for name, (base, spread) in spreads.items():
        noise = np.random.default_rng([zlib.crc32(name.encode()), seed]).standard_normal(out[name].shape)
        drawn = base * np.exp(spread * noise) if base else spread * noise
        out[name] = jnp.asarray(drawn.astype(out[name].dtype))
    for name, factor in factors.items():
        out[name] = (out[name] * factor).astype(out[name].dtype)
    return out
```

```python
from contextlib import ExitStack

import numpy as np
import concourse.bass as bass
from concourse import mybir
from concourse.alu_op_type import AluOpType as ALU

F32 = mybir.dt.float32
F32R = mybir.dt.float32r
U32 = mybir.dt.uint32
ACT = mybir.ActivationFunctionType

P = 128
D = 512
KT = D // P
E, R = 8, 16
ER = E * R
AG = ER + E
DFF = 2048
NF = DFF // P
TOKENS = 4096
SEQ = 1024
CHUNK = 512
TPC = CHUNK // P
NCH = TOKENS // CHUNK
CPS = SEQ // CHUNK
LN_EPS = 1e-5
RMS_EPS = 1.1920929e-07
SUM_EPS = 1e-6

O_AG = 0
O_B = O_AG + KT * AG
O_W = O_B + D
O_K = O_W + KT * D
O_V = O_K + KT * D
O_Q = O_V + KT * D
RES = O_Q + KT * D
PIECES = 8
PIECE = RES // PIECES
assert PIECE * PIECES == RES and PIECES % 2 == 0
REC = 2 * D + D
PART = 512

SLOTS = {
    0: ["T1"], 2: ["AG1"], 3: ["SK", "LN3"], 4: ["TG1"], 5: ["T3"], 6: ["WB1"], 7: ["AG3"], 8: ["T2"],
    9: ["TG3"], 10: ["K"], 11: ["V"], 12: ["Q"], 13: ["TW", "LN1"], 14: ["TWV", "TE"], 15: ["WB3", "Y"],
}
STAGE1 = ("SK", "LN1", "T1", "AG1", "TG1", "WB1", "T2", "K", "V", "Q", "TW", "TWV", "TE", "Y")
STAGE3 = ("LN3", "T3", "AG3", "TG3", "WB3")


def chunk_items(with1, with3, first=False):
    for f in range(NF):
        t = f // TPC
        if f == 0:
            main = [[] if first else ["out_a"], [] if first else ["out_b"], ["gate"], ["up"]]
        elif f == 1 and first:
            main = [["gate"], ["out_a"], ["up"], ["out_b"]]
        else:
            main = [["gate"], ["out_a"], ["up"], ["out_b"]]
        for q in range(4):
            for name in main[q]:
                yield name, f, t
            if q < 3:
                yield f"split{q}", f, t
            for name in SLOTS.get(4 * (f % TPC) + q, ()):
                if (name in STAGE1 and with1) or (name in STAGE3 and with3) or (name == "SK" and t == 0):
                    yield name, f, t


def build_program(nc, x, resident, stream, half_bias, gate_bias, consts, out):
    with ExitStack() as ctx:
        def sb(name, shape, dt=F32):
            return ctx.enter_context(nc.sbuf_tensor(name, shape, dt))

        def bank(name):
            return ctx.enter_context(nc.psum_tensor(name, [P, 512], F32))

        def sem(name):
            return ctx.enter_context(nc.semaphore(name))

        res_hi, res_lo = sb("res_hi", [P, RES], F32R), sb("res_lo", [P, RES], F32R)
        raw = [sb(f"raw{i}", [P, REC]) for i in range(2)]
        rec_hi = [sb(f"rec_hi{i}", [P, REC], F32R) for i in range(2)]
        rec_lo = [sb(f"rec_lo{i}", [P, REC], F32R) for i in range(2)]
        bias_raw = sb("bias_raw", [P, D])
        gbias = sb("gbias", [P, E])
        const = sb("const", [P, 2 * P + E])
        ident, ones, iota = const[:, 0:P], const[:, P:2 * P], const[:, 2 * P:2 * P + E]
        minus_half = sb("minus_half", [P, 2])
        x0 = [sb(f"x0_{i}", [P, D]) for i in range(2)]
        x1 = sb("x1", [P, D])
        skip = [[sb(f"skip{p}_{t}", [P, D]) for t in range(TPC)] for p in range(2)]
        y_hi = [sb(f"y_hi{p}", [P, KT, CHUNK], F32R) for p in range(2)]
        y_lo = [sb(f"y_lo{p}", [P, KT, CHUNK], F32R) for p in range(2)]
        w_tok, wv_tok, eq_tok = sb("w_tok", [P, D]), sb("wv_tok", [P, D]), sb("eq_tok", [P, D])
        cum_w, cum_wv, yf = sb("cum_w", [P, D]), sb("cum_wv", [P, D]), sb("yf", [P, D])
        carry_w, carry_wv = sb("carry_w", [P, KT]), sb("carry_wv", [P, KT])
        hid = sb("hid", [P, CHUNK])
        h_hi = [sb(f"h_hi{i}", [P, CHUNK], F32R) for i in range(2)]
        h_lo = [sb(f"h_lo{i}", [P, CHUNK], F32R) for i in range(2)]
        norm = {k: sb(f"norm{k}", [P, D]) for k in (1, 2, 3)}
        xt_hi = {k: sb(f"xt_hi{k}", [P, D], F32R) for k in (1, 2, 3)}
        xt_lo = {k: sb(f"xt_lo{k}", [P, D], F32R) for k in (1, 2, 3)}
        bn6 = {k: sb(f"bn6_{k}", [P, 6]) for k in (1, 2, 3)}
        mv = {k: sb(f"mv{k}", [P, 2]) for k in (1, 2, 3)}
        ve = {k: sb(f"ve{k}", [P, 2]) for k in (1, 2, 3)}
        rs = {k: sb(f"rs{k}", [P, 2]) for k in (1, 2, 3)}
        skip_ab = sb("skip_ab", [P, 2])
        lg = {k: sb(f"lg{k}", [P, E]) for k in (1, 3)}
        top = {k: sb(f"top{k}", [P, 8]) for k in (1, 3)}
        idx = {k: sb(f"idx{k}", [P, 8], U32) for k in (1, 3)}
        idxf = {k: sb(f"idxf{k}", [P, 2]) for k in (1, 3)}
        ex = {k: sb(f"ex{k}", [P, 1]) for k in (1, 3)}
        gden = {k: sb(f"gden{k}", [P, 1]) for k in (1, 3)}
        gts = {k: sb(f"gts{k}", [P, 2]) for k in (1, 3)}
        pick = {k: sb(f"pick{k}", [P, 2, E]) for k in (1, 3)}
        gt = {k: sb(f"gt{k}", [P, E]) for k in (1, 3)}
        gated = {k: sb(f"gated{k}", [P, ER]) for k in (1, 3)}
        gt_hi = {k: sb(f"gt_hi{k}", [P, P], F32R) for k in (1, 3)}
        gt_lo = {k: sb(f"gt_lo{k}", [P, P], F32R) for k in (1, 3)}
        qk_sum = {k: sb(f"{k}_sum", [P, 1]) for k in "kq"}
        qk_ms = {k: sb(f"{k}_ms", [P, 1]) for k in "kq"}
        qk_r = {k: sb(f"{k}_r", [P, 1]) for k in "kq"}
        q_neg = sb("q_neg", [P, 1])

        bank_g, bank_u = bank("bank_g"), bank("bank_u")
        bank_o = [bank(f"bank_o{t}") for t in range(TPC)]
        bank_x = [bank("bank_x0"), bank("bank_x1")]
        BANK = {"T1": 0, "AG1": 0, "TG1": 0, "WB1": 0, "T2": 0, "K": 0, "V": 1, "Q": 0, "TW": 1,
                "TWV": 0, "TE": 1, "T3": 1, "AG3": 1, "TG3": 1, "WB3": 1}

        S = {}
        for name in (
            "const_loaded", "bias_ready", "const_ready", "res_hi_ready", "res_lo_ready",
            "rec_hi_ready", "rec_lo_ready",
            "stats1", "stats2", "stats3", "rstd1", "rstd2", "rstd3", "norm1", "norm2", "norm3",
            "t1_done", "t2_done", "t3_done", "xt_hi1", "xt_hi2", "xt_hi3", "xt_lo1", "xt_lo2", "xt_lo3",
            "ag1_done", "ag3_done", "top1", "top3", "ex1", "ex3", "gated1", "gated3",
            "tg1_done", "tg3_done", "gt_hi1", "gt_hi3", "gt_lo1", "gt_lo3", "wb1_done", "wb3_done",
            "resid1", "resid3", "skip_ready", "x1_ready", "x3_ready",
            "k_done", "k_sum", "k_scale", "w_ready", "v_done", "wv_ready", "q_done", "q_sum", "q_scale",
            "eq_ready", "tw_done", "twv_done", "te_done", "cumw_ready", "cumwv_ready", "den_ready",
            "yf_ready", "yhi_ready", "ylo_ready",
            "g_done", "u_done", "tanh_ready", "h_ready", "hhi_ready", "hlo_ready", "out_done",
            "x2_ready",
            "ln1_order", "ln2_order", "ln3_order", "gate1_order", "gate3_order", "sum_order", "y_order",
            "h_order", "pool1_order", "pool2_order", "pool3_order", "poolk_order", "poolq_order",
        ):
            S[name] = sem(name)
        raw_loaded = [sem("raw0_loaded"), sem("raw1_loaded")]
        x_loaded = [sem("x0_loaded"), sem("x1_loaded")]
        out_stored = [sem(f"out_stored{t}") for t in range(TPC)]

        def after(eng, name, count):
            if not (isinstance(count, int) and count <= 0):
                eng.wait_ge(S[name], count)

        def apart(eng):
            eng.nop(nofuse=True)

        class Order:

            def __init__(self, eng, name, per, n):
                self.eng, self.sem, self.per, self.n, self.done = eng, S[name], per, n, 0

            def __call__(self, ins):
                ins.then_inc(self.sem, 1)
                self.done += 1
                assert self.done <= self.per
                self.eng.wait_ge(self.sem, self.n * self.per + self.done)

            def end(self):
                assert self.done == self.per, (self.done, self.per)

        def f32(ap):
            return ap.bitcast(F32)

        def sp_load_record(sp, f, ring):
            sp.dma_start(raw[ring][:, :], stream[f % NF]).then_inc(raw_loaded[ring], 16)

        def sp_item(sp, name, f, t, c, last):
            j, m = c + 1, 4 * (c - 1) + t
            if name == "gate" and not (last and f == NF - 1):
                after(sp, "rec_hi_ready", 3 * (NF * c + f + 1))
                after(sp, "rec_lo_ready", 3 * (NF * c + f + 1))
                sp_load_record(sp, f + 2, f % 2)
            elif name == "T1":
                sp_load_x(sp, 4 * j + t, t)
            elif name == "WB3":
                sp_store(sp, m, t, (c - 1) if isinstance(c, int) else None, PAR[0])

        def sp_load_x(sp, n, t):
            after(sp, "x1_ready", n)
            sp.dma_start(x0[(t + 1) % 2][:, :], x[bass.ds((n + 1) * P, P), :]).then_inc(x_loaded[(t + 1) % 2], 16)

        PAR = [0]

        def sp_store(sp, m, t, _, par):
            after(sp, "x3_ready", m + 1)
            sp.dma_start(out[bass.ds(m * P, P), :], skip[par][t][:, :]).then_inc(out_stored[t], 16)

        def mm3(pe, acc, st_hi, st_lo, mv_hi, mv_lo, start, stop):
            pe.matmul(acc, st_hi, mv_hi, start=start, stop=False)
            pe.matmul(acc, st_hi, mv_lo, start=False, stop=False)
            return pe.matmul(acc, st_lo, mv_hi, start=False, stop=stop)

        def pe_transpose4(pe, b, src):
            for kt in range(KT):
                last = pe.transpose(b[:, kt * P:(kt + 1) * P], src[:, kt * P:(kt + 1) * P], ident)
            return last

        def pe_from_x(pe, k, acc, o, width, stop=True):
            for kt in range(KT):
                a, b = o + kt * width, o + (kt + 1) * width
                cols = slice(kt * P, (kt + 1) * P)
                last = mm3(pe, acc, xt_hi[k][:, cols], xt_lo[k][:, cols], res_hi[:, a:b], res_lo[:, a:b],
                           kt == 0, stop and kt == KT - 1)
            return last

        def res_need(end):
            return -(-end // PIECE)

        def pe_item(pe, name, f, t, c, par):
            n, m, F = 4 * (c + 1) + t, 4 * (c - 1) + t, NF * c + f
            ring = f % 2
            if name == "gate":
                if f == 0:
                    after(pe, "ylo_ready", 4 * (c + 1))
                after(pe, "rec_lo_ready", 3 * F + 1)
                after(pe, "h_ready", F)
                for kt in range(KT):
                    cols = slice(kt * P, (kt + 1) * P)
                    last = mm3(pe, bank_g[:, :], rec_hi[ring][:, cols], rec_lo[ring][:, cols],
                               y_hi[par][:, kt, :], y_lo[par][:, kt, :], kt == 0, kt == KT - 1)
                last.then_inc(S["g_done"], 1)
            elif name == "up":
                after(pe, "rec_lo_ready", 3 * F + 2)
                for kt in range(KT):
                    cols = slice(D + kt * P, D + (kt + 1) * P)
                    last = mm3(pe, bank_u[:, :], rec_hi[ring][:, cols], rec_lo[ring][:, cols],
                               y_hi[par][:, kt, :], y_lo[par][:, kt, :], kt == 0, kt == KT - 1)
                last.then_inc(S["u_done"], 1)
            elif name in ("out_a", "out_b"):
                if name == "out_a":
                    after(pe, "rec_lo_ready", 3 * F + 3)
                    after(pe, "hlo_ready", F)
                    if f == 1:
                        after(pe, "x2_ready", 4 * c)
                for t2 in ((0, 1) if name == "out_a" else (2, 3)):
                    cols = slice(t2 * P, (t2 + 1) * P)
                    last = mm3(pe, bank_o[t2][:, :], h_hi[1 - ring][:, cols], h_lo[1 - ring][:, cols],
                               rec_hi[ring][:, 2 * D:REC], rec_lo[ring][:, 2 * D:REC], f == 1, f == 0)
                last.then_inc(S["out_done"], 1)
            elif name in STAGE1:
                pe_stage1(pe, name, n, m)
            elif name in STAGE3:
                pe_stage3(pe, name, n, m)

        def pe_stage1(pe, name, n, m):
            if name not in BANK:
                return
            b = bank_x[BANK[name]]
            if name == "T1":
                after(pe, "cumwv_ready", n)
                after(pe, "norm1", n + 1)
                pe_transpose4(pe, b, norm[1]).then_inc(S["t1_done"], 1)
            elif name == "AG1":
                pe.wait_ge(S["res_lo_ready"], res_need(O_B))
                after(pe, "xt_lo1", n + 1)
                pe_from_x(pe, 1, b[:, 0:AG], O_AG, AG).then_inc(S["ag1_done"], 1)
            elif name == "TG1":
                after(pe, "gated1", n + 1)
                pe.transpose(b[:, 0:P], gated[1][:, :], ident).then_inc(S["tg1_done"], 1)
            elif name == "WB1":
                pe.wait_ge(S["res_lo_ready"], res_need(O_K))
                after(pe, "gt_lo1", n + 1)
                pe_from_x(pe, 1, b[:, :], O_W, D, stop=False)
                mm3(pe, b[:, :], gt_hi[1][:, :], gt_lo[1][:, :], res_hi[:, O_B:O_W], res_lo[:, O_B:O_W],
                    False, True).then_inc(S["wb1_done"], 1)
            elif name == "T2":
                after(pe, "norm2", n + 1)
                pe_transpose4(pe, b, norm[2]).then_inc(S["t2_done"], 1)
            elif name == "K":
                pe.wait_ge(S["res_lo_ready"], res_need(O_V))
                after(pe, "xt_lo2", n + 1)
                pe_from_x(pe, 2, b[:, :], O_K, D).then_inc(S["k_done"], 1)
            elif name == "V":
                pe.wait_ge(S["res_lo_ready"], res_need(O_Q))
                after(pe, "den_ready", n)
                if not (isinstance(m, int) and m < 0):
                    after(pe, "gt_lo3", m + 1)
                pe_from_x(pe, 2, b[:, :], O_V, D).then_inc(S["v_done"], 1)
            elif name == "Q":
                pe.wait_ge(S["res_lo_ready"], PIECES)
                after(pe, "w_ready", n + 1)
                pe_from_x(pe, 2, b[:, :], O_Q, D).then_inc(S["q_done"], 1)
            elif name == "TW":
                after(pe, "wv_ready", n + 1)
                pe_transpose4(pe, b, w_tok).then_inc(S["tw_done"], 1)
            elif name == "TWV":
                after(pe, "eq_ready", n + 1)
                pe_transpose4(pe, b, wv_tok).then_inc(S["twv_done"], 1)
            elif name == "TE":
                after(pe, "cumw_ready", n + 1)
                pe_transpose4(pe, b, eq_tok).then_inc(S["te_done"], 1)

        def pe_stage3(pe, name, n, m):
            if name not in BANK:
                return
            b = bank_x[BANK[name]]
            den = n if not isinstance(n, int) else min(n, TPC * NCH)
            if name == "T3":
                after(pe, "den_ready", den)
                after(pe, "x3_ready", m)
                after(pe, "norm3", m + 1)
                pe_transpose4(pe, b, norm[3]).then_inc(S["t3_done"], 1)
            elif name == "AG3":
                after(pe, "xt_lo3", m + 1)
                pe_from_x(pe, 3, b[:, 0:AG], O_AG, AG).then_inc(S["ag3_done"], 1)
            elif name == "TG3":
                after(pe, "gated3", m + 1)
                pe.transpose(b[:, 0:P], gated[3][:, :], ident).then_inc(S["tg3_done"], 1)
            elif name == "WB3":
                if not (isinstance(n, int) and n >= TPC * NCH):
                    after(pe, "den_ready", n + 1)
                after(pe, "gt_lo3", m + 1)
                pe_from_x(pe, 3, b[:, :], O_W, D, stop=False)
                mm3(pe, b[:, :], gt_hi[3][:, :], gt_lo[3][:, :], res_hi[:, O_B:O_W], res_lo[:, O_B:O_W],
                    False, True).then_inc(S["wb3_done"], 1)

        def act_item(act, name, f, t, c, par):
            n, m, F = 4 * (c + 1) + t, 4 * (c - 1) + t, NF * c + f
            ring = f % 2
            if name == "gate":
                after(act, "g_done", F + 1)
                after(act, "hlo_ready", F)
                act.activation(hid[:, :], bank_g[:, :], ACT.Tanh, scale=0.5).then_inc(S["tanh_ready"], 1)
            elif name == "up":
                after(act, "h_ready", F + 1)
                after(act, "out_done", 2 * (F - 1))
                act.activation(h_hi[ring][:, :], hid[:, :], ACT.Copy).then_inc(S["hhi_ready"], 1)
            elif name.startswith("split"):
                split_hi(act, int(name[-1]), 1 - ring, f + 1, F + 1, c)
            elif name in STAGE1:
                act_stage1(act, name, n, t, c, 1 - par)
            elif name in STAGE3:
                act_ffn(act, name, 3, m)

        def split_wait_ring(eng, part, F):
            if part == 0:
                after(eng, "g_done", F - 1)
            elif part == 1:
                after(eng, "u_done", F - 1)
            else:
                after(eng, "out_done", 2 * (F - 2))

        def raw_count(f, c):
            return 16 * (PIECES // 2 + NF // 2 * c + f // 2 + 1)

        def split_hi(act, part, ring, f, F, c):
            cols = slice(part * PART, (part + 1) * PART)
            if part == 0:
                act.wait_ge(raw_loaded[ring], raw_count(f, c))
            split_wait_ring(act, part, F)
            act.activation(rec_hi[ring][:, cols], raw[ring][:, cols], ACT.Copy).then_inc(S["rec_hi_ready"], 1)

        def act_ffn(act, name, k, n):
            if name == f"T{k}":
                after(act, f"t{k}_done", n + 1)
                after(act, f"wb{k}_done", n)
                act.activation(xt_hi[k][:, :], bank_x[BANK[name]][:, :], ACT.Copy).then_inc(S[f"xt_hi{k}"], 1)
            elif name == f"AG{k}":
                after(act, f"top{k}", n + 1)
                act.activation(ex[k][:, :], top[k][:, 0:1], ACT.Exp, bias=top[k][:, 1:2],
                               scale=-1.0).then_inc(S[f"ex{k}"], 1)
            elif name == f"TG{k}":
                after(act, f"tg{k}_done", n + 1)
                act.activation(gt_hi[k][:, :], bank_x[BANK[name]][:, 0:P], ACT.Copy).then_inc(S[f"gt_hi{k}"], 1)

        def act_stage1(act, name, n, t, c, par):
            act_ffn(act, name, 1, n)
            if name == "T2":
                after(act, "t2_done", n + 1)
                after(act, "q_done", n)
                act.activation(xt_hi[2][:, :], bank_x[0][:, :], ACT.Copy).then_inc(S["xt_hi2"], 1)
            elif name in ("K", "Q"):
                k = name.lower()
                dst, gone, ready, sign = ((w_tok, "tw_done", "w_ready", 1) if k == "k" else
                                          (eq_tok, "te_done", "eq_ready", -1))
                after(act, f"{k}_done", n + 1)
                after(act, gone, n)
                act.activation(dst[:, :], bank_x[BANK[name]][:, :], ACT.Square,
                               accum_out=qk_sum[k][:, :]).then_inc(S[f"{k}_sum"], 1)
                after(act, f"{k}_scale", n + 1)
                act.activation(dst[:, :], bank_x[BANK[name]][:, :], ACT.Exp,
                               scale=(qk_r["k"] if sign > 0 else q_neg)[:, 0:1]).then_inc(S[ready], 1)
            elif name == "Y":
                after(act, "yf_ready", n + 1)
                after(act, "u_done", NF * c)
                act.activation(y_hi[par][:, :, t * P:(t + 1) * P], yf[:, :].rearrange("p (k m) -> p k m", k=KT),
                               ACT.Copy).then_inc(S["yhi_ready"], 1)

        def dve_item(dve, name, f, t, c, par):
            n, m, F = 4 * (c + 1) + t, 4 * (c - 1) + t, NF * c + f
            ring = f % 2
            if name == "gate":
                after(dve, "tanh_ready", F + 1)
                o = Order(dve, "h_order", 1, F)
                o(dve.scalar_tensor_tensor(out=hid[:, :], in0=hid[:, :], scalar=1.0, in1=bank_g[:, :],
                                           op0=ALU.add, op1=ALU.mult))
                o.end()
            elif name == "up":
                after(dve, "u_done", F + 1)
                dve.tensor_tensor(hid[:, :], hid[:, :], bank_u[:, :], ALU.mult).then_inc(S["h_ready"], 1)
                after(dve, "hhi_ready", F + 1)
                dve.tensor_tensor(h_lo[ring][:, :], hid[:, :], f32(h_hi[ring][:, :]),
                                  ALU.subtract).then_inc(S["hlo_ready"], 1)
            elif name in ("out_a", "out_b"):
                if f == 0:
                    after(dve, "out_done", 2 * F - (1 if name == "out_a" else 0))
                    after(dve, "skip_ready", NF // 4 * c)
                    for t2 in ((0, 1) if name == "out_a" else (2, 3)):
                        sk = skip[1 - par][t2]
                        dve.scalar_tensor_tensor(out=sk[:, :], in0=bank_o[t2][:, :], scalar=0.5, in1=sk[:, :],
                                                 op0=ALU.mult, op1=ALU.add).then_inc(S["x2_ready"], 1)
            elif name.startswith("split"):
                split_lo(dve, int(name[-1]), 1 - ring, F + 1)
            elif name in STAGE1:
                dve_stage1(dve, name, n, t, c, 1 - par)
            elif name in STAGE3:
                dve_stage3(dve, name, m, t, 1 - par)

        def split_lo(dve, part, ring, F):
            cols = slice(part * PART, (part + 1) * PART)
            after(dve, "rec_hi_ready", 3 * F + part + 1)
            split_wait_ring(dve, part, F)
            dve.tensor_tensor(rec_lo[ring][:, cols], raw[ring][:, cols], f32(rec_hi[ring][:, cols]),
                              ALU.subtract).then_inc(S["rec_lo_ready"], 1)

        def dve_ffn(dve, name, k, n):
            if name == f"T{k}":
                after(dve, f"xt_hi{k}", n + 1)
                dve.tensor_tensor(xt_lo[k][:, :], bank_x[BANK[name]][:, :], f32(xt_hi[k][:, :]),
                                  ALU.subtract).then_inc(S[f"xt_lo{k}"], 1)
            elif name == f"AG{k}":
                b = bank_x[BANK[name]]
                o = Order(dve, f"gate{k}_order", 8, n)
                after(dve, f"ag{k}_done", n + 1)
                o(dve.tensor_tensor(lg[k][:, :], b[:, ER:AG], gbias[:, :], ALU.add))
                apart(dve)
                o(dve.max(top[k][:, :], lg[k][:, :]))
                apart(dve)
                dve.max_index(idx[k][:, :], top[k][:, :], lg[k][:, :]).then_inc(S[f"top{k}"], 1)
                after(dve, f"top{k}", n + 1)
                o(dve.tensor_copy(idxf[k][:, :], idx[k][:, 0:2]))
                after(dve, f"ex{k}", n + 1)
                o(dve.tensor_scalar(gden[k][:, :], ex[k][:, :], 1.0, None, ALU.add))
                o(dve.reciprocal(gts[k][:, 0:1], gden[k][:, :]))
                o(dve.tensor_tensor(gts[k][:, 1:2], gts[k][:, 0:1], ex[k][:, :], ALU.mult))
                dve.tensor_scalar(pick[k][:, 0, :], iota, idxf[k][:, 0:1], gts[k][:, 0:1], ALU.is_equal, ALU.mult)
                o(dve.tensor_scalar(pick[k][:, 1, :], iota, idxf[k][:, 1:2], gts[k][:, 1:2],
                                    ALU.is_equal, ALU.mult))
                o(dve.tensor_tensor(gt[k][:, :], pick[k][:, 0, :], pick[k][:, 1, :], ALU.add))
                o.end()
                after(dve, f"tg{k}_done", n)
                dve.tensor_tensor(gated[k][:, :].rearrange("p (e r) -> p e r", e=E),
                                  b[:, 0:ER].rearrange("p (e r) -> p e r", e=E),
                                  gt[k][:, :].unsqueeze(2).to_broadcast([P, E, R]),
                                  ALU.mult).then_inc(S[f"gated{k}"], 1)
            elif name == f"TG{k}":
                after(dve, f"gt_hi{k}", n + 1)
                dve.tensor_tensor(gt_lo[k][:, :], bank_x[BANK[name]][:, 0:P], f32(gt_hi[k][:, :]),
                                  ALU.subtract).then_inc(S[f"gt_lo{k}"], 1)

        def dve_ln1(dve, n, t):
            o = Order(dve, "ln1_order", 1, n)
            dve.wait_ge(x_loaded[t % 2], XCOUNT(n, t))
            o(dve.bn_stats(bn6[1][:, :], x0[t % 2][:, :]))
            apart(dve)
            dve.bn_aggr(mv[1][:, :], bn6[1][:, :]).then_inc(S["stats1"], 1)
            after(dve, "rstd1", n + 1)
            after(dve, "t1_done", n)
            dve.tensor_scalar(norm[1][:, :], x0[t % 2][:, :], mv[1][:, 0:1], rs[1][:, 0:1],
                              ALU.subtract, ALU.mult).then_inc(S["norm1"], 1)

        def XCOUNT(n, t):
            return 8 * (n - t % 2) + 16

        def dve_stage1(dve, name, n, t, c, par):
            j = c + 1
            if name == "LN1":
                dve_ln1(dve, n + 1, (t + 1) % TPC)
            dve_ffn(dve, name, 1, n)
            if name == "WB1":
                o = Order(dve, "ln2_order", 1, n)
                after(dve, "wb1_done", n + 1)
                after(dve, "resid1", n + 1)
                dve.scalar_tensor_tensor(out=x1[:, :], in0=bank_x[0][:, :], scalar=0.5, in1=x0[t % 2][:, :],
                                         op0=ALU.mult, op1=ALU.add).then_inc(S["x1_ready"], 1)
                after(dve, "x1_ready", n + 1)
                o(dve.bn_stats(bn6[2][:, :], x1[:, :]))
                apart(dve)
                dve.bn_aggr(mv[2][:, :], bn6[2][:, :]).then_inc(S["stats2"], 1)
                after(dve, "rstd2", n + 1)
                after(dve, "t2_done", n)
                dve.tensor_scalar(norm[2][:, :], x1[:, :], mv[2][:, 0:1], rs[2][:, 1:2],
                                  ALU.subtract, ALU.mult).then_inc(S["norm2"], 1)
                o.end()
            elif name == "SK":
                chunk, par_s, t_s = (j, par, t - 1) if t else (c, 1 - par, TPC - 1)
                if not (isinstance(chunk, int) and chunk < 2):
                    dve.wait_ge(out_stored[t_s], 16 * (chunk - 1))
                dve.tensor_scalar(skip[par_s][t_s][:, :], x1[:, :], skip_ab[:, 0:1], skip_ab[:, 1:2],
                                  ALU.mult, ALU.subtract).then_inc(S["skip_ready"], 1)
            elif name == "T2":
                after(dve, "xt_hi2", n + 1)
                dve.tensor_tensor(xt_lo[2][:, :], bank_x[0][:, :], f32(xt_hi[2][:, :]),
                                  ALU.subtract).then_inc(S["xt_lo2"], 1)
            elif name == "V":
                after(dve, "v_done", n + 1)
                after(dve, "w_ready", n + 1)
                after(dve, "twv_done", n)
                dve.tensor_tensor(wv_tok[:, :], w_tok[:, :], bank_x[1][:, :], ALU.mult).then_inc(S["wv_ready"], 1)
            elif name == "TW":
                after(dve, "tw_done", n + 1)
                dve_scan(dve, n, 0, cum_w, carry_w, bank_x[1], SUM_EPS, t == 0 and par % CPS == 0, "cumw_ready")
            elif name == "TE":
                after(dve, "te_done", n + 1)
                o = Order(dve, "y_order", 1, n)
                dve.scalar_tensor_tensor(out=yf[:, :], in0=bank_x[1][:, :], scalar=1.0, in1=cum_w[:, :],
                                         op0=ALU.add, op1=ALU.mult).then_inc(S["den_ready"], 1)
                after(dve, "den_ready", n + 1)
                o(dve.reciprocal(yf[:, :], yf[:, :]))
                after(dve, "twv_done", n + 1)
                dve_scan(dve, n, 1, cum_wv, carry_wv, bank_x[0], 0.0, t == 0 and par % CPS == 0, "cumwv_ready")
                dve.tensor_tensor(yf[:, :], yf[:, :], cum_wv[:, :], ALU.mult).then_inc(S["yf_ready"], 1)
                o.end()
            elif name == "Y":
                after(dve, "yhi_ready", n + 1)
                dve.tensor_tensor(y_lo[par][:, :, t * P:(t + 1) * P], yf[:, :].rearrange("p (k m) -> p k m", k=KT),
                                  f32(y_hi[par][:, :, t * P:(t + 1) * P]), ALU.subtract).then_inc(S["ylo_ready"], 1)

        def dve_scan(dve, n, which, cum, carry, b, start, fresh, ready):
            for kt in range(KT):
                cols = slice(kt * P, (kt + 1) * P)
                last = dve.tensor_tensor_scan(cum[:, cols], ones, b[:, cols],
                                              start if fresh else carry[:, kt:kt + 1], ALU.mult, ALU.add)
            last.then_inc(S[ready], 1)
            dve.wait_ge(S[ready], n + 1)
            dve.tensor_copy(carry[:, :].unsqueeze(2),
                            cum[:, :].rearrange("p (k m) -> p k m", k=KT)[:, :, P - 1:P]).then_inc(S["sum_order"], 1)
            dve.wait_ge(S["sum_order"], 2 * n + which + 1)

        def dve_stage3(dve, name, m, t, par):
            sk = skip[par][t]
            if name == "LN3":
                o = Order(dve, "ln3_order", 1, m)
                after(dve, "x2_ready", m + 1)
                o(dve.bn_stats(bn6[3][:, :], sk[:, :]))
                apart(dve)
                dve.bn_aggr(mv[3][:, :], bn6[3][:, :]).then_inc(S["stats3"], 1)
                after(dve, "rstd3", m + 1)
                after(dve, "t3_done", m)
                dve.tensor_scalar(norm[3][:, :], sk[:, :], mv[3][:, 0:1], rs[3][:, 0:1],
                                  ALU.subtract, ALU.mult).then_inc(S["norm3"], 1)
            dve_ffn(dve, name, 3, m)
            if name == "WB3":
                after(dve, "wb3_done", m + 1)
                after(dve, "resid3", m + 1)
                dve.scalar_tensor_tensor(out=sk[:, :], in0=bank_x[1][:, :], scalar=0.5, in1=sk[:, :],
                                         op0=ALU.mult, op1=ALU.add).then_inc(S["x3_ready"], 1)

        def pool_item(pool, name, f, t, c, par):
            n, m = 4 * (c + 1) + t, 4 * (c - 1) + t
            if name in STAGE1:
                pool_stage1(pool, name, n, t)
            elif name == "LN3":
                pool_rstd(pool, 3, m)
            elif name == "T3":
                after(pool, "norm3", m + 1)
                sk = skip[1 - par][t]
                pool.tensor_tensor(sk[:, :], sk[:, :], bias_raw[:, :], ALU.add).then_inc(S["resid3"], 1)

        def pool_rstd(pool, k, n):
            o = Order(pool, f"pool{k}_order", 1, n)
            after(pool, f"stats{k}", n + 1)
            apart(pool)
            o(pool.tensor_scalar(ve[k][:, 0:1], mv[k][:, 1:2], LN_EPS, 1.0, ALU.add, ALU.mult))
            pool.tensor_tensor(rs[k][:, 0:1], ve[k][:, 0:1], minus_half[:, 0:1], ALU.pow).then_inc(S[f"rstd{k}"], 1)

        def pool_stage1(pool, name, n, t):
            if name == "LN1":
                pool_rstd(pool, 1, n + 1)
            elif name == "T1":
                after(pool, "norm1", n + 1)
                x = x0[t % 2]
                pool.tensor_tensor(x[:, :], x[:, :], bias_raw[:, :], ALU.add).then_inc(S["resid1"], 1)
            elif name == "WB1":
                o = Order(pool, "pool2_order", 2, n)
                after(pool, "stats2", n + 1)
                apart(pool)
                pool.tensor_scalar(ve[2][:, 0:1], mv[2][:, 1:2], LN_EPS, 1.0, ALU.add, ALU.mult)
                apart(pool)
                o(pool.tensor_scalar(ve[2][:, 1:2], mv[2][:, 1:2], 1.0 + RMS_EPS, RMS_EPS * LN_EPS,
                                     ALU.mult, ALU.add))
                o(pool.tensor_tensor(rs[2][:, :], ve[2][:, :], minus_half[:, :], ALU.pow))
                apart(pool)
                pool.tensor_scalar(skip_ab[:, 0:1], rs[2][:, 0:1], 1.0, 1.0, ALU.add, ALU.mult)
                pool.tensor_tensor(skip_ab[:, 1:2], rs[2][:, 0:1], mv[2][:, 0:1], ALU.mult).then_inc(S["rstd2"], 1)
                o.end()
            elif name in ("K", "Q"):
                k = name.lower()
                o = Order(pool, f"pool{k}_order", 1 if k == "k" else 2, n)
                after(pool, f"{k}_sum", n + 1)
                apart(pool)
                o(pool.tensor_scalar(qk_ms[k][:, :], qk_sum[k][:, :], 1.0 / D, RMS_EPS, ALU.mult, ALU.add))
                root = pool.tensor_tensor(qk_r[k][:, :], qk_ms[k][:, :], minus_half[:, 0:1], ALU.pow)
                if k == "k":
                    root.then_inc(S["k_scale"], 1)
                else:
                    o(root)
                    apart(pool)
                    pool.tensor_scalar(q_neg[:, :], qk_r[k][:, :], -1.0, 1.0, ALU.mult, ALU.mult)\
                        .then_inc(S["q_scale"], 1)
                o.end()

        def whole(eng, item, fori):
            for t in range(TPC):
                if t:
                    item(eng, "SK", -1, t, -1, 1)
                for name in ("T1", "AG1", "TG1", "WB1", "T2", "K", "V", "Q", "TW", "TWV", "TE", "Y", "LN1"):
                    item(eng, name, -1, t, -1, 1)
            if item is act_item or item is dve_item:
                for part in range(3):
                    item(eng, f"split{part}", -1, TPC - 1, 0, 1)
            def chunk(c, par, **which):
                for name, f, t in chunk_items(**which):
                    item(eng, name, f, t, c, par)

            chunk(0, 0, with1=True, with3=False, first=True)
            chunk(1, 1, with1=True, with3=True)
            with fori(0, (NCH - 4) // 2) as pair:
                chunk(pair * 2 + 2, 0, with1=True, with3=True)
                chunk(pair * 2 + 3, 1, with1=True, with3=True)
            chunk(NCH - 2, 0, with1=True, with3=True)
            chunk(NCH - 1, 1, with1=False, with3=True)
            for name in ("out_a", "out_b"):
                item(eng, name, 0, 0, NCH, 0)
            for t in range(TPC):
                for name in ("LN3", "T3", "AG3", "TG3", "WB3"):
                    item(eng, name, 0, t, NCH, 0)

        block = ctx.enter_context(nc.Block())

        @block.sync
        def _(sp):
            def item(sp, name, f, t, c, par):
                PAR[0] = 1 - par
                sp_item(sp, name, f, t, c, isinstance(c, int) and c == NCH - 1)

            sp.dma_start(x0[0][:, :], x[0:P, :]).then_inc(x_loaded[0], 16)
            sp.dma_start(const[:, :], consts).then_inc(S["const_loaded"], 16)
            sp.dma_start(bias_raw[:, :], half_bias).then_inc(S["const_loaded"], 16)
            sp.dma_start(gbias[:, :], gate_bias).then_inc(S["const_loaded"], 16)
            for i in range(PIECES):
                after(sp, "res_hi_ready", i - 1)
                after(sp, "res_lo_ready", i - 1)
                sp.dma_start(raw[i % 2][:, 0:PIECE], resident[i]).then_inc(raw_loaded[i % 2], 16)
            for i in range(2):
                after(sp, "res_hi_ready", PIECES - 1 + i)
                after(sp, "res_lo_ready", PIECES - 1 + i)
                sp_load_record(sp, i, i)
            whole(sp, item, sp.Fori)
            for t in range(TPC):
                sp.wait_ge(out_stored[t], 16 * NCH)

        @block.gpsimd
        def _(pool):
            pool.memset(minus_half[:, :], -0.5).then_inc(S["const_ready"], 1)
            pool.wait_ge(S["const_ready"], 1)
            pool.wait_ge(S["bias_ready"], 1)
            pool_rstd(pool, 1, 0)
            whole(pool, pool_item, pool.Fori)

        @block.scalar
        def _(act):
            for i in range(PIECES):
                cols = slice(i * PIECE, (i + 1) * PIECE)
                act.wait_ge(raw_loaded[i % 2], 16 * (i // 2 + 1))
                act.activation(res_hi[:, cols], raw[i % 2][:, 0:PIECE], ACT.Copy).then_inc(S["res_hi_ready"], 1)
            whole(act, act_item, act.Fori)

        @block.vector
        def _(dve):
            dve.wait_ge(S["const_loaded"], 48)
            dve.tensor_scalar(bias_raw[:, :], bias_raw[:, :], 0.5, None, ALU.mult).then_inc(S["bias_ready"], 1)
            dve_ln1(dve, 0, 0)
            for i in range(PIECES):
                cols = slice(i * PIECE, (i + 1) * PIECE)
                after(dve, "res_hi_ready", i + 1)
                dve.tensor_tensor(res_lo[:, cols], raw[i % 2][:, 0:PIECE], f32(res_hi[:, cols]),
                                  ALU.subtract).then_inc(S["res_lo_ready"], 1)
            whole(dve, dve_item, dve.Fori)

        @block.tensor
        def _(pe):
            pe.wait_ge(S["const_loaded"], 48)
            whole(pe, pe_item, pe.Fori)


def kernel(L0_attn_x, L0_attn_w_qkv, L0_attn_w_swiglu, L0_attn_w_out, L0_ffn_W, L0_ffn_b, L0_ffn_lora_A,
           L0_ffn_lora_B, L0_ffn_gate_w, L0_ffn_gate_b):
    import concourse.bacc as bacc
    from concourse.bass_utils import run_bass_kernel_spmd

    def arr(a):
        return np.asarray(a)

    def by_k(w):
        o, i = w.shape
        return w.T.reshape(i // P, P, o).transpose(1, 0, 2).reshape(P, -1)

    xs = arr(L0_attn_x).reshape(TOKENS, D)
    ag = np.concatenate([arr(L0_ffn_lora_A).reshape(ER, D), arr(L0_ffn_gate_w)], 0)
    lora_b = arr(L0_ffn_lora_B).transpose(0, 2, 1).reshape(ER, D)
    wq, wk, wv = (arr(L0_attn_w_qkv)[i * D:(i + 1) * D] for i in range(3))
    resident = np.concatenate([by_k(ag), lora_b, by_k(arr(L0_ffn_W)), by_k(wk), by_k(wv), by_k(wq)], 1)
    resident = np.ascontiguousarray(resident.reshape(P, PIECES, PIECE).transpose(1, 0, 2))
    up, gate = arr(L0_attn_w_swiglu)[:DFF], arr(L0_attn_w_swiglu)[DFF:]
    w_out = arr(L0_attn_w_out).T
    stream = np.stack([
        np.concatenate([by_k(gate[f * P:(f + 1) * P]), by_k(up[f * P:(f + 1) * P]),
                        w_out[(f - 1) % NF * P:((f - 1) % NF + 1) * P]], 1) for f in range(NF)])
    arrays = {
        "x_rows": np.ascontiguousarray(np.concatenate([xs, xs[:P]], 0)),
        "resident": resident,
        "stream": np.ascontiguousarray(stream),
        "bias": np.ascontiguousarray(np.broadcast_to(arr(L0_ffn_b), (P, D))),
        "gate_bias": np.ascontiguousarray(np.broadcast_to(arr(L0_ffn_gate_b), (P, E))),
        "consts": np.concatenate([np.eye(P, dtype=np.float32), np.ones((P, P), np.float32),
                                  np.tile(np.arange(E, dtype=np.float32), (P, 1))], 1),
    }
    nc = bacc.Bacc("TRN2", target_bir_lowering=False, num_devices=1, dynamic_dma_scratch_size=8192)
    args = [nc.dram_tensor(name, a.shape, F32, kind="ExternalInput").ap() for name, a in arrays.items()]
    out = nc.dram_tensor("out_rows", (TOKENS, D), F32, kind="ExternalOutput").ap()
    build_program(nc, *args, out)
    got = run_bass_kernel_spmd(nc, [arrays], core_ids=[0]).results[0]["out_rows"]
    return got.reshape(L0_attn_x.shape)
```

```python
from contextlib import ExitStack

import numpy as np
import concourse.bass as bass
from concourse import mybir
from concourse.alu_op_type import AluOpType as ALU

F32 = mybir.dt.float32
F32R = mybir.dt.float32r
U32 = mybir.dt.uint32
ACT = mybir.ActivationFunctionType

P = 128
D = 512
KT = D // P
E, R = 8, 16
ER = E * R
AG = ER + E
DFF = 2048
NF = DFF // P
TOKENS = 4096
SEQ = 1024
CHUNK = 512
TPC = CHUNK // P
NCH = TOKENS // CHUNK
CPS = SEQ // CHUNK
LN_EPS = 1e-5
RMS_EPS = 1.1920929e-07
SUM_EPS = 1e-6

O_AG = 0
O_B = O_AG + KT * AG
O_W = O_B + D
O_K = O_W + KT * D
O_V = O_K + KT * D
O_Q = O_V + KT * D
RES = O_Q + KT * D
PIECES = 8
PIECE = RES // PIECES
assert PIECE * PIECES == RES and PIECES % 2 == 0
REC = 2 * D + D
PART = 512

STEPS = (
    "gate act_gate T1 out_a LN3a hi0 hi1 hi2 lo0 lo1 lo2 up act_up AG1 low out_b SK LN3b",
    "gate act_gate TG1 out_a T3 hi0 hi1 hi2 lo0 lo1 lo2 up act_up low WB1 out_b LN2b AG3",
    "gate act_gate T2 out_a hi0 hi1 hi2 lo0 lo1 lo2 up act_up low TG3 K V out_b Q LN1a",
    "gate act_gate TW out_a TWV hi0 hi1 hi2 lo0 lo1 up act_up TE lo2 low out_b LN1b RA RB Y WB3",
)
FIRST_STEP = "out_a T1 out_b hi0 hi1 hi2 lo0 lo1 gate act_gate AG1 up act_up lo2 low LN3a SK LN3b"
STAGE1 = ("SK", "LN1a", "LN1b", "T1", "AG1", "TG1", "WB1", "LN2b", "T2", "K", "V", "Q", "TW", "TWV", "TE",
          "RA", "RB", "Y")
STAGE3 = ("LN3a", "LN3b", "T3", "AG3", "TG3", "WB3")


def chunk_items(with1, with3, first=False):
    for f in range(NF):
        for name in (STEPS[f % TPC] if f else FIRST_STEP).split():
            if name in STAGE1 and not with1 and not (name == "SK" and f == 0):
                continue
            if name in STAGE3 and not with3 or first and f == 0 and name in ("out_a", "out_b"):
                continue
            yield name, f, f // TPC


def build_program(nc, x, resident, stream, half_bias, gate_bias, consts, out):
    with ExitStack() as ctx:
        def sb(name, shape, dt=F32):
            return ctx.enter_context(nc.sbuf_tensor(name, shape, dt))

        def bank(name):
            return ctx.enter_context(nc.psum_tensor(name, [P, 512], F32))

        def sem(name):
            return ctx.enter_context(nc.semaphore(name))

        res_hi, res_lo = sb("res_hi", [P, RES], F32R), sb("res_lo", [P, RES], F32R)
        raw = [sb(f"raw{i}", [P, REC]) for i in range(2)]
        rec_hi = [sb(f"rec_hi{i}", [P, REC], F32R) for i in range(2)]
        rec_lo = [sb(f"rec_lo{i}", [P, REC], F32R) for i in range(2)]
        bias_raw = sb("bias_raw", [P, D])
        gbias = sb("gbias", [P, E])
        const = sb("const", [P, 2 * P + E])
        ident, ones, iota = const[:, 0:P], const[:, P:2 * P], const[:, 2 * P:2 * P + E]
        minus_half = sb("minus_half", [P, 2])
        x0 = [sb(f"x0_{i}", [P, D]) for i in range(2)]
        x1 = sb("x1", [P, D])
        skip = [[sb(f"skip{p}_{t}", [P, D]) for t in range(TPC)] for p in range(2)]
        y_hi = [sb(f"y_hi{p}", [P, KT, CHUNK], F32R) for p in range(2)]
        y_lo = [sb(f"y_lo{p}", [P, KT, CHUNK], F32R) for p in range(2)]
        w_tok, wv_tok, eq_tok = sb("w_tok", [P, D]), sb("wv_tok", [P, D]), sb("eq_tok", [P, D])
        cum_w, cum_wv, yf = sb("cum_w", [P, D]), sb("cum_wv", [P, D]), sb("yf", [P, D])
        carry_w, carry_wv = sb("carry_w", [P, KT]), sb("carry_wv", [P, KT])
        hid = sb("hid", [P, CHUNK])
        h_hi = [sb(f"h_hi{i}", [P, CHUNK], F32R) for i in range(2)]
        h_lo = [sb(f"h_lo{i}", [P, CHUNK], F32R) for i in range(2)]
        norm = {k: sb(f"norm{k}", [P, D]) for k in (1, 2, 3)}
        xt_hi = {k: sb(f"xt_hi{k}", [P, D], F32R) for k in (1, 2, 3)}
        xt_lo = {k: sb(f"xt_lo{k}", [P, D], F32R) for k in (1, 2, 3)}
        bn6 = {k: sb(f"bn6_{k}", [P, 6]) for k in (1, 2, 3)}
        mv = {k: sb(f"mv{k}", [P, 2]) for k in (1, 2, 3)}
        ve = {k: sb(f"ve{k}", [P, 2]) for k in (1, 2, 3)}
        rs = {k: sb(f"rs{k}", [P, 2]) for k in (1, 2, 3)}
        skip_ab = sb("skip_ab", [P, 2])
        lg = {k: sb(f"lg{k}", [P, E]) for k in (1, 3)}
        top = {k: sb(f"top{k}", [P, 8]) for k in (1, 3)}
        idx = {k: sb(f"idx{k}", [P, 8], U32) for k in (1, 3)}
        idxf = {k: sb(f"idxf{k}", [P, 2]) for k in (1, 3)}
        ex = {k: sb(f"ex{k}", [P, 1]) for k in (1, 3)}
        gden = {k: sb(f"gden{k}", [P, 1]) for k in (1, 3)}
        gts = {k: sb(f"gts{k}", [P, 2]) for k in (1, 3)}
        pick = {k: sb(f"pick{k}", [P, 2, E]) for k in (1, 3)}
        gt = {k: sb(f"gt{k}", [P, E]) for k in (1, 3)}
        gated = {k: sb(f"gated{k}", [P, ER]) for k in (1, 3)}
        gt_hi = {k: sb(f"gt_hi{k}", [P, P], F32R) for k in (1, 3)}
        gt_lo = {k: sb(f"gt_lo{k}", [P, P], F32R) for k in (1, 3)}
        qk_sum = {k: sb(f"{k}_sum", [P, 1]) for k in "kq"}
        qk_ms = {k: sb(f"{k}_ms", [P, 1]) for k in "kq"}
        qk_r = {k: sb(f"{k}_r", [P, 1]) for k in "kq"}
        q_neg = sb("q_neg", [P, 1])

        bank_g, bank_u = bank("bank_g"), bank("bank_u")
        bank_o = [bank(f"bank_o{t}") for t in range(TPC)]
        bank_x = [bank("bank_x0"), bank("bank_x1")]
        x0_, x1_ = bank_x
        BANK = {"T1": x0_, "AG1": x0_, "TG1": x0_, "WB1": x0_, "T2": x0_, "K": x0_, "V": x1_, "Q": x0_,
                "TW": x1_, "TWV": x0_, "TE": x1_, "T3": x1_, "AG3": x1_, "TG3": x1_, "WB3": x1_}
        EARLY = dict(BANK, T1=bank_o[0], AG1=bank_o[1], TG1=bank_o[2], WB1=bank_o[3], T2=bank_g, K=bank_u,
                     TW=bank_g, TWV=bank_u)

        def side_bank(name, f):
            return (EARLY if f < 0 else BANK)[name]

        S = {}
        for name in (
            "const_loaded", "bias_ready", "const_ready", "res_hi_ready", "res_lo_ready",
            "rec_hi_ready", "rec_lo_ready",
            "stats1", "stats2", "stats3", "rstd1", "rstd2", "rstd3", "norm1", "norm2", "norm3",
            "t1_done", "t2_done", "t3_done", "xt_hi1", "xt_hi2", "xt_hi3", "xt_lo1", "xt_lo2", "xt_lo3",
            "ag1_done", "ag3_done", "top1", "top3", "ex1", "ex3", "gated1", "gated3",
            "tg1_done", "tg3_done", "gt_hi1", "gt_hi3", "gt_lo1", "gt_lo3", "wb1_done", "wb3_done",
            "resid1", "resid3", "skip_ab_ready", "skip_ready", "x1_ready", "x3_ready",
            "k_done", "k_sum", "k_scale", "w_ready", "v_done", "wv_ready", "q_done", "q_sum", "q_scale",
            "eq_ready", "tw_done", "twv_done", "te_done", "cumw_ready", "cumwv_ready", "den_ready",
            "yf_ready", "yhi_ready", "ylo_ready",
            "g_done", "u_done", "tanh_ready", "gate_used", "h_ready", "hhi_ready", "hlo_ready", "out_done",
            "x2_ready",
            "ln1_order", "ln2_order", "ln3_order", "gate1_order", "gate3_order", "sum_order", "y_order",
            "pool1_order", "pool2_order", "pool3_order", "poolk_order", "poolq_order",
        ):
            S[name] = sem(name)
        raw_loaded = [sem("raw0_loaded"), sem("raw1_loaded")]
        x_loaded = [sem("x0_loaded"), sem("x1_loaded")]
        out_stored = [sem(f"out_stored{t}") for t in range(TPC)]

        def after(eng, name, count):
            if not (isinstance(count, int) and count <= 0):
                eng.wait_ge(S[name], count)

        def apart(eng):
            eng.nop(nofuse=True)

        class Order:

            def __init__(self, eng, name, per, n):
                self.eng, self.sem, self.per, self.n, self.done = eng, S[name], per, n, 0

            def __call__(self, ins):
                ins.then_inc(self.sem, 1)
                self.done += 1
                assert self.done <= self.per
                self.eng.wait_ge(self.sem, self.n * self.per + self.done)

            def end(self):
                assert self.done == self.per, (self.done, self.per)

        def f32(ap):
            return ap.bitcast(F32)

        def sp_load_record(sp, f, ring):
            sp.dma_start(raw[ring][:, :], stream[f % NF]).then_inc(raw_loaded[ring], 16)

        def sp_item(sp, name, f, t, c, last):
            j, m = c + 1, 4 * (c - 1) + t
            if name == "gate" and not (last and f == NF - 1):
                after(sp, "rec_hi_ready", 3 * (NF * c + f + 1))
                after(sp, "rec_lo_ready", 3 * (NF * c + f + 1))
                sp_load_record(sp, f + 2, f % 2)
            elif name == "T1" and not (f < 0 and t == 0):
                sp_load_x(sp, 4 * j + t, t)
            elif name == "WB3":
                sp_store(sp, m, t, (c - 1) if isinstance(c, int) else None, PAR[0])

        def sp_load_x(sp, n, t):
            after(sp, "x1_ready", n)
            sp.dma_start(x0[(t + 1) % 2][:, :], x[bass.ds((n + 1) * P, P), :]).then_inc(x_loaded[(t + 1) % 2], 16)

        PAR = [0]

        def sp_store(sp, m, t, _, par):
            after(sp, "x3_ready", m + 1)
            sp.dma_start(out[bass.ds(m * P, P), :], skip[par][t][:, :]).then_inc(out_stored[t], 16)

        def mm3(pe, acc, st_hi, st_lo, mv_hi, mv_lo, start, stop):
            pe.matmul(acc, st_hi, mv_hi, start=start, stop=False)
            pe.matmul(acc, st_hi, mv_lo, start=False, stop=False)
            return pe.matmul(acc, st_lo, mv_hi, start=False, stop=stop)

        def pe_transpose4(pe, b, src):
            for kt in range(KT):
                last = pe.transpose(b[:, kt * P:(kt + 1) * P], src[:, kt * P:(kt + 1) * P], ident)
            return last

        def pe_from_x(pe, k, acc, o, width, stop=True):
            for kt in range(KT):
                a, b = o + kt * width, o + (kt + 1) * width
                cols = slice(kt * P, (kt + 1) * P)
                last = mm3(pe, acc, xt_hi[k][:, cols], xt_lo[k][:, cols], res_hi[:, a:b], res_lo[:, a:b],
                           kt == 0, stop and kt == KT - 1)
            return last

        def res_need(end):
            return -(-end // PIECE)

        def pe_item(pe, name, f, t, c, par):
            n, m, F = 4 * (c + 1) + t, 4 * (c - 1) + t, NF * c + f
            ring = f % 2
            if name == "gate":
                if f == 0:
                    after(pe, "ylo_ready", 4 * (c + 1))
                after(pe, "rec_lo_ready", 3 * F + 1)
                after(pe, "gate_used", F)
                for kt in range(KT):
                    cols = slice(kt * P, (kt + 1) * P)
                    last = mm3(pe, bank_g[:, :], rec_hi[ring][:, cols], rec_lo[ring][:, cols],
                               y_hi[par][:, kt, :], y_lo[par][:, kt, :], kt == 0, kt == KT - 1)
                last.then_inc(S["g_done"], 1)
            elif name == "up":
                after(pe, "rec_lo_ready", 3 * F + 2)
                after(pe, "h_ready", F)
                for kt in range(KT):
                    cols = slice(D + kt * P, D + (kt + 1) * P)
                    last = mm3(pe, bank_u[:, :], rec_hi[ring][:, cols], rec_lo[ring][:, cols],
                               y_hi[par][:, kt, :], y_lo[par][:, kt, :], kt == 0, kt == KT - 1)
                last.then_inc(S["u_done"], 1)
            elif name in ("out_a", "out_b"):
                if name == "out_a":
                    after(pe, "rec_lo_ready", 3 * F + 3)
                    after(pe, "hlo_ready", F)
                    if f == 1:
                        after(pe, "x2_ready", 4 * c)
                for t2 in ((0, 1) if name == "out_a" else (2, 3)):
                    cols = slice(t2 * P, (t2 + 1) * P)
                    last = mm3(pe, bank_o[t2][:, :], h_hi[1 - ring][:, cols], h_lo[1 - ring][:, cols],
                               rec_hi[ring][:, 2 * D:REC], rec_lo[ring][:, 2 * D:REC], f == 1, f == 0)
                last.then_inc(S["out_done"], 1)
            elif name in STAGE1:
                pe_stage1(pe, name, n, m, f)
            elif name in STAGE3:
                pe_stage3(pe, name, n, m)

        def pe_stage1(pe, name, n, m, f):
            if name not in BANK:
                return
            b = side_bank(name, f)
            if name == "T1":
                if f >= 0:
                    after(pe, "cumwv_ready", n)
                after(pe, "norm1", n + 1)
                pe_transpose4(pe, b, norm[1]).then_inc(S["t1_done"], 1)
            elif name == "AG1":
                pe.wait_ge(S["res_lo_ready"], res_need(O_B))
                after(pe, "xt_lo1", n + 1)
                pe_from_x(pe, 1, b[:, 0:AG], O_AG, AG).then_inc(S["ag1_done"], 1)
            elif name == "TG1":
                after(pe, "gated1", n + 1)
                pe.transpose(b[:, 0:P], gated[1][:, :], ident).then_inc(S["tg1_done"], 1)
            elif name == "WB1":
                pe.wait_ge(S["res_lo_ready"], res_need(O_K))
                after(pe, "gt_lo1", n + 1)
                pe_from_x(pe, 1, b[:, :], O_W, D, stop=False)
                mm3(pe, b[:, :], gt_hi[1][:, :], gt_lo[1][:, :], res_hi[:, O_B:O_W], res_lo[:, O_B:O_W],
                    False, True).then_inc(S["wb1_done"], 1)
            elif name == "T2":
                after(pe, "norm2", n + 1)
                pe_transpose4(pe, b, norm[2]).then_inc(S["t2_done"], 1)
            elif name == "K":
                pe.wait_ge(S["res_lo_ready"], res_need(O_V))
                after(pe, "xt_lo2", n + 1)
                after(pe, "cumwv_ready", n)
                pe_from_x(pe, 2, b[:, :], O_K, D).then_inc(S["k_done"], 1)
            elif name == "V":
                pe.wait_ge(S["res_lo_ready"], res_need(O_Q))
                after(pe, "den_ready", n)
                if not (isinstance(m, int) and m < 0):
                    after(pe, "gt_lo3", m + 1)
                pe_from_x(pe, 2, b[:, :], O_V, D).then_inc(S["v_done"], 1)
            elif name == "Q":
                pe.wait_ge(S["res_lo_ready"], PIECES)
                after(pe, "w_ready", n + 1)
                pe_from_x(pe, 2, b[:, :], O_Q, D).then_inc(S["q_done"], 1)
            elif name == "TW":
                after(pe, "wv_ready", n + 1)
                pe_transpose4(pe, b, w_tok).then_inc(S["tw_done"], 1)
            elif name == "TWV":
                if f >= 0:
                    after(pe, "eq_ready", n + 1)
                pe_transpose4(pe, b, wv_tok).then_inc(S["twv_done"], 1)
            elif name == "TE":
                after(pe, "cumw_ready", n + 1)
                if f < 0:
                    after(pe, "eq_ready", n + 1)
                pe_transpose4(pe, b, eq_tok).then_inc(S["te_done"], 1)

        def pe_stage3(pe, name, n, m):
            if name not in BANK:
                return
            b = BANK[name]
            den = n if not isinstance(n, int) else min(n, TPC * NCH)
            if name == "T3":
                after(pe, "den_ready", den)
                after(pe, "x3_ready", m)
                after(pe, "norm3", m + 1)
                pe_transpose4(pe, b, norm[3]).then_inc(S["t3_done"], 1)
            elif name == "AG3":
                after(pe, "xt_lo3", m + 1)
                pe_from_x(pe, 3, b[:, 0:AG], O_AG, AG).then_inc(S["ag3_done"], 1)
            elif name == "TG3":
                after(pe, "gated3", m + 1)
                pe.transpose(b[:, 0:P], gated[3][:, :], ident).then_inc(S["tg3_done"], 1)
            elif name == "WB3":
                if not (isinstance(n, int) and n >= TPC * NCH):
                    after(pe, "den_ready", n + 1)
                after(pe, "gt_lo3", m + 1)
                pe_from_x(pe, 3, b[:, :], O_W, D, stop=False)
                mm3(pe, b[:, :], gt_hi[3][:, :], gt_lo[3][:, :], res_hi[:, O_B:O_W], res_lo[:, O_B:O_W],
                    False, True).then_inc(S["wb3_done"], 1)

        def act_item(act, name, f, t, c, par):
            n, m, F = 4 * (c + 1) + t, 4 * (c - 1) + t, NF * c + f
            ring = f % 2
            if name == "gate":
                after(act, "g_done", F + 1)
                after(act, "hlo_ready", F)
                act.activation(hid[:, :], bank_g[:, :], ACT.Tanh, scale=0.5).then_inc(S["tanh_ready"], 1)
            elif name == "act_up":
                after(act, "h_ready", F + 1)
                after(act, "out_done", 2 * (F - 1))
                act.activation(h_hi[ring][:, :], hid[:, :], ACT.Copy).then_inc(S["hhi_ready"], 1)
            elif name in ("hi0", "hi1", "hi2"):
                split_hi(act, int(name[-1]), 1 - ring, f + 1, F + 1, c)
            elif name in STAGE1:
                act_stage1(act, name, n, t, c, 1 - par, f)
            elif name in STAGE3:
                act_ffn(act, name, 3, m, f)
            elif name.startswith("res"):
                i = int(name[3:])
                cols = slice(i * PIECE, (i + 1) * PIECE)
                act.wait_ge(raw_loaded[i % 2], 16 * (i // 2 + 1))
                act.activation(res_hi[:, cols], raw[i % 2][:, 0:PIECE], ACT.Copy).then_inc(S["res_hi_ready"], 1)

        def split_wait_ring(eng, part, F):
            if part == 0:
                after(eng, "g_done", F - 1)
            elif part == 1:
                after(eng, "u_done", F - 1)
            else:
                after(eng, "out_done", 2 * (F - 2))

        def raw_count(f, c):
            return 16 * (PIECES // 2 + NF // 2 * c + f // 2 + 1)

        def split_hi(act, part, ring, f, F, c):
            cols = slice(part * PART, (part + 1) * PART)
            if part == 0:
                act.wait_ge(raw_loaded[ring], raw_count(f, c))
            split_wait_ring(act, part, F)
            act.activation(rec_hi[ring][:, cols], raw[ring][:, cols], ACT.Copy).then_inc(S["rec_hi_ready"], 1)

        def act_ffn(act, name, k, n, f):
            if name == f"T{k}":
                after(act, f"t{k}_done", n + 1)
                after(act, f"wb{k}_done", n)
                act.activation(xt_hi[k][:, :], side_bank(name, f)[:, :], ACT.Copy).then_inc(S[f"xt_hi{k}"], 1)
            elif name == f"AG{k}":
                after(act, f"top{k}", n + 1)
                act.activation(ex[k][:, :], top[k][:, 0:1], ACT.Exp, bias=top[k][:, 1:2],
                               scale=-1.0).then_inc(S[f"ex{k}"], 1)
            elif name == f"TG{k}":
                after(act, f"tg{k}_done", n + 1)
                act.activation(gt_hi[k][:, :], side_bank(name, f)[:, 0:P], ACT.Copy).then_inc(S[f"gt_hi{k}"], 1)

        def act_stage1(act, name, n, t, c, par, f):
            act_ffn(act, name, 1, n, f)
            if name == "T2":
                after(act, "t2_done", n + 1)
                after(act, "q_done", n)
                act.activation(xt_hi[2][:, :], side_bank(name, f)[:, :], ACT.Copy).then_inc(S["xt_hi2"], 1)
            elif name in ("K", "Q"):
                k = name.lower()
                dst, gone, ready, sign = ((w_tok, "tw_done", "w_ready", 1) if k == "k" else
                                          (eq_tok, "te_done", "eq_ready", -1))
                after(act, f"{k}_done", n + 1)
                after(act, gone, n)
                act.activation(dst[:, :], side_bank(name, f)[:, :], ACT.Square,
                               accum_out=qk_sum[k][:, :]).then_inc(S[f"{k}_sum"], 1)
                after(act, f"{k}_scale", n + 1)
                act.activation(dst[:, :], side_bank(name, f)[:, :], ACT.Exp,
                               scale=(qk_r["k"] if sign > 0 else q_neg)[:, 0:1]).then_inc(S[ready], 1)
            elif name == "Y":
                after(act, "yf_ready", n + 1)
                after(act, "u_done", NF * c)
                act.activation(y_hi[par][:, :, t * P:(t + 1) * P], yf[:, :].rearrange("p (k m) -> p k m", k=KT),
                               ACT.Copy).then_inc(S["yhi_ready"], 1)

        def dve_item(dve, name, f, t, c, par):
            n, m, F = 4 * (c + 1) + t, 4 * (c - 1) + t, NF * c + f
            ring = f % 2
            if name == "act_gate":
                after(dve, "tanh_ready", F + 1)
                o = Order(dve, "gate_used", 1, F)
                o(dve.scalar_tensor_tensor(out=hid[:, :], in0=hid[:, :], scalar=1.0, in1=bank_g[:, :],
                                           op0=ALU.add, op1=ALU.mult))
                o.end()
            elif name == "act_up":
                after(dve, "u_done", F + 1)
                dve.tensor_tensor(hid[:, :], hid[:, :], bank_u[:, :], ALU.mult).then_inc(S["h_ready"], 1)
            elif name == "low":
                after(dve, "hhi_ready", F + 1)
                dve.tensor_tensor(h_lo[ring][:, :], hid[:, :], f32(h_hi[ring][:, :]),
                                  ALU.subtract).then_inc(S["hlo_ready"], 1)
            elif name in ("out_a", "out_b"):
                if f == 0:
                    after(dve, "out_done", 2 * F - (1 if name == "out_a" else 0))
                    after(dve, "skip_ready", NF // 4 * c)
                    for t2 in ((0, 1) if name == "out_a" else (2, 3)):
                        sk = skip[1 - par][t2]
                        dve.scalar_tensor_tensor(out=sk[:, :], in0=bank_o[t2][:, :], scalar=0.5, in1=sk[:, :],
                                                 op0=ALU.mult, op1=ALU.add).then_inc(S["x2_ready"], 1)
            elif name in ("lo0", "lo1", "lo2"):
                split_lo(dve, int(name[-1]), 1 - ring, F + 1)
            elif name in STAGE1:
                dve_stage1(dve, name, n, t, c, 1 - par, f)
            elif name in STAGE3:
                dve_stage3(dve, name, m, t, 1 - par, f)
            elif name.startswith("res"):
                i = int(name[3:])
                cols = slice(i * PIECE, (i + 1) * PIECE)
                after(dve, "res_hi_ready", i + 1)
                dve.tensor_tensor(res_lo[:, cols], raw[i % 2][:, 0:PIECE], f32(res_hi[:, cols]),
                                  ALU.subtract).then_inc(S["res_lo_ready"], 1)

        def split_lo(dve, part, ring, F):
            cols = slice(part * PART, (part + 1) * PART)
            after(dve, "rec_hi_ready", 3 * F + part + 1)
            split_wait_ring(dve, part, F)
            dve.tensor_tensor(rec_lo[ring][:, cols], raw[ring][:, cols], f32(rec_hi[ring][:, cols]),
                              ALU.subtract).then_inc(S["rec_lo_ready"], 1)

        def dve_ffn(dve, name, k, n, f):
            if name == f"T{k}":
                after(dve, f"xt_hi{k}", n + 1)
                dve.tensor_tensor(xt_lo[k][:, :], side_bank(name, f)[:, :], f32(xt_hi[k][:, :]),
                                  ALU.subtract).then_inc(S[f"xt_lo{k}"], 1)
            elif name == f"AG{k}":
                b = side_bank(name, f)
                o = Order(dve, f"gate{k}_order", 8, n)
                after(dve, f"ag{k}_done", n + 1)
                o(dve.tensor_tensor(lg[k][:, :], b[:, ER:AG], gbias[:, :], ALU.add))
                apart(dve)
                o(dve.max(top[k][:, :], lg[k][:, :]))
                apart(dve)
                dve.max_index(idx[k][:, :], top[k][:, :], lg[k][:, :]).then_inc(S[f"top{k}"], 1)
                after(dve, f"top{k}", n + 1)
                o(dve.tensor_copy(idxf[k][:, :], idx[k][:, 0:2]))
                after(dve, f"ex{k}", n + 1)
                o(dve.tensor_scalar(gden[k][:, :], ex[k][:, :], 1.0, None, ALU.add))
                o(dve.reciprocal(gts[k][:, 0:1], gden[k][:, :]))
                o(dve.tensor_tensor(gts[k][:, 1:2], gts[k][:, 0:1], ex[k][:, :], ALU.mult))
                dve.tensor_scalar(pick[k][:, 0, :], iota, idxf[k][:, 0:1], gts[k][:, 0:1], ALU.is_equal, ALU.mult)
                o(dve.tensor_scalar(pick[k][:, 1, :], iota, idxf[k][:, 1:2], gts[k][:, 1:2],
                                    ALU.is_equal, ALU.mult))
                o(dve.tensor_tensor(gt[k][:, :], pick[k][:, 0, :], pick[k][:, 1, :], ALU.add))
                o.end()
                after(dve, f"tg{k}_done", n)
                dve.tensor_tensor(gated[k][:, :].rearrange("p (e r) -> p e r", e=E),
                                  b[:, 0:ER].rearrange("p (e r) -> p e r", e=E),
                                  gt[k][:, :].unsqueeze(2).to_broadcast([P, E, R]),
                                  ALU.mult).then_inc(S[f"gated{k}"], 1)
            elif name == f"TG{k}":
                after(dve, f"gt_hi{k}", n + 1)
                dve.tensor_tensor(gt_lo[k][:, :], side_bank(name, f)[:, 0:P], f32(gt_hi[k][:, :]),
                                  ALU.subtract).then_inc(S[f"gt_lo{k}"], 1)

        def dve_stats(dve, k, n, src):
            o = Order(dve, f"ln{k}_order", 1, n)
            o(dve.bn_stats(bn6[k][:, :], src))
            apart(dve)
            dve.bn_aggr(mv[k][:, :], bn6[k][:, :]).then_inc(S[f"stats{k}"], 1)

        def dve_norm(dve, k, n, src):
            after(dve, f"rstd{k}", n + 1)
            after(dve, f"t{k}_done", n)
            col = 1 if k == 2 else 0
            dve.tensor_scalar(norm[k][:, :], src, mv[k][:, 0:1], rs[k][:, col:col + 1],
                              ALU.subtract, ALU.mult).then_inc(S[f"norm{k}"], 1)

        def XCOUNT(n, t):
            return 8 * (n - t % 2) + 16

        def dve_stage1(dve, name, n, t, c, par, f):
            j = c + 1
            x_next = x0[(t + 1) % 2][:, :]
            dve_ffn(dve, name, 1, n, f)
            if name == "LN1a":
                dve.wait_ge(x_loaded[(t + 1) % 2], XCOUNT(n + 1, t + 1))
                dve_stats(dve, 1, n + 1, x_next)
            elif name == "LN1b":
                dve_norm(dve, 1, n + 1, x_next)
            if name == "WB1":
                after(dve, "wb1_done", n + 1)
                after(dve, "resid1", n + 1)
                dve.scalar_tensor_tensor(out=x1[:, :], in0=side_bank(name, f)[:, :], scalar=0.5, in1=x0[t % 2][:, :],
                                         op0=ALU.mult, op1=ALU.add).then_inc(S["x1_ready"], 1)
                after(dve, "x1_ready", n + 1)
                dve_stats(dve, 2, n, x1[:, :])
            elif name == "LN2b":
                dve_norm(dve, 2, n, x1[:, :])
            elif name == "SK":
                chunk, par_s, t_s = (j, par, t - 1) if t else (c, 1 - par, TPC - 1)
                if not (isinstance(chunk, int) and chunk < 2):
                    dve.wait_ge(out_stored[t_s], 16 * (chunk - 1))
                after(dve, "skip_ab_ready", n)
                apart(dve)
                dve.tensor_scalar(skip[par_s][t_s][:, :], x1[:, :], skip_ab[:, 0:1], skip_ab[:, 1:2],
                                  ALU.mult, ALU.subtract).then_inc(S["skip_ready"], 1)
            elif name == "T2":
                after(dve, "xt_hi2", n + 1)
                dve.tensor_tensor(xt_lo[2][:, :], side_bank(name, f)[:, :], f32(xt_hi[2][:, :]),
                                  ALU.subtract).then_inc(S["xt_lo2"], 1)
            elif name == "V":
                after(dve, "v_done", n + 1)
                after(dve, "w_ready", n + 1)
                after(dve, "twv_done", n)
                dve.tensor_tensor(wv_tok[:, :], w_tok[:, :], side_bank(name, f)[:, :], ALU.mult).then_inc(S["wv_ready"], 1)
            elif name == "TW":
                after(dve, "tw_done", n + 1)
                dve_scan(dve, n, 0, cum_w, carry_w, side_bank(name, f), SUM_EPS, t == 0 and par % CPS == 0, "cumw_ready")
            elif name == "TWV":
                after(dve, "twv_done", n + 1)
                dve_scan(dve, n, 1, cum_wv, carry_wv, side_bank(name, f), 0.0, t == 0 and par % CPS == 0,
                         "cumwv_ready")
            elif name == "TE":
                after(dve, "te_done", n + 1)
                dve.scalar_tensor_tensor(out=yf[:, :], in0=side_bank(name, f)[:, :], scalar=1.0, in1=cum_w[:, :],
                                         op0=ALU.add, op1=ALU.mult).then_inc(S["den_ready"], 1)
            elif name == "RA":
                after(dve, "den_ready", n + 1)
                dve.reciprocal(yf[:, 0:D // 2], yf[:, 0:D // 2])
            elif name == "RB":
                o = Order(dve, "y_order", 1, n)
                o(dve.reciprocal(yf[:, D // 2:D], yf[:, D // 2:D]))
                dve.tensor_tensor(yf[:, :], yf[:, :], cum_wv[:, :], ALU.mult).then_inc(S["yf_ready"], 1)
                o.end()
            elif name == "Y":
                after(dve, "yhi_ready", n + 1)
                dve.tensor_tensor(y_lo[par][:, :, t * P:(t + 1) * P], yf[:, :].rearrange("p (k m) -> p k m", k=KT),
                                  f32(y_hi[par][:, :, t * P:(t + 1) * P]), ALU.subtract).then_inc(S["ylo_ready"], 1)

        def dve_scan(dve, n, which, cum, carry, b, start, fresh, ready):
            for kt in range(KT):
                cols = slice(kt * P, (kt + 1) * P)
                last = dve.tensor_tensor_scan(cum[:, cols], ones, b[:, cols],
                                              start if fresh else carry[:, kt:kt + 1], ALU.mult, ALU.add)
            last.then_inc(S[ready], 1)
            dve.wait_ge(S[ready], n + 1)
            dve.tensor_copy(carry[:, :].unsqueeze(2),
                            cum[:, :].rearrange("p (k m) -> p k m", k=KT)[:, :, P - 1:P]).then_inc(S["sum_order"], 1)
            dve.wait_ge(S["sum_order"], 2 * n + which + 1)

        def dve_stage3(dve, name, m, t, par, f):
            sk = skip[par][t]
            if name == "LN3a":
                after(dve, "x2_ready", m + 1)
                dve_stats(dve, 3, m, sk[:, :])
            elif name == "LN3b":
                dve_norm(dve, 3, m, sk[:, :])
            dve_ffn(dve, name, 3, m, f)
            if name == "WB3":
                after(dve, "wb3_done", m + 1)
                after(dve, "resid3", m + 1)
                dve.scalar_tensor_tensor(out=sk[:, :], in0=BANK[name][:, :], scalar=0.5, in1=sk[:, :],
                                         op0=ALU.mult, op1=ALU.add).then_inc(S["x3_ready"], 1)

        def pool_item(pool, name, f, t, c, par):
            n, m = 4 * (c + 1) + t, 4 * (c - 1) + t
            if name in STAGE1:
                pool_stage1(pool, name, n, t)
            elif name == "LN3a":
                pool_rstd(pool, 3, m)
            elif name == "T3":
                after(pool, "norm3", m + 1)
                sk = skip[1 - par][t]
                pool.tensor_tensor(sk[:, :], sk[:, :], bias_raw[:, :], ALU.add).then_inc(S["resid3"], 1)

        def pool_rstd(pool, k, n):
            o = Order(pool, f"pool{k}_order", 1, n)
            after(pool, f"stats{k}", n + 1)
            apart(pool)
            o(pool.tensor_scalar(ve[k][:, 0:1], mv[k][:, 1:2], LN_EPS, 1.0, ALU.add, ALU.mult))
            pool.tensor_tensor(rs[k][:, 0:1], ve[k][:, 0:1], minus_half[:, 0:1], ALU.pow).then_inc(S[f"rstd{k}"], 1)

        def pool_stage1(pool, name, n, t):
            if name == "LN1a":
                pool_rstd(pool, 1, n + 1)
            elif name == "T1":
                after(pool, "norm1", n + 1)
                x = x0[t % 2]
                pool.tensor_tensor(x[:, :], x[:, :], bias_raw[:, :], ALU.add).then_inc(S["resid1"], 1)
            elif name == "WB1":
                o = Order(pool, "pool2_order", 1, n)
                after(pool, "stats2", n + 1)
                apart(pool)
                pool.tensor_scalar(ve[2][:, 0:1], mv[2][:, 1:2], LN_EPS, 1.0, ALU.add, ALU.mult)
                apart(pool)
                o(pool.tensor_scalar(ve[2][:, 1:2], mv[2][:, 1:2], 1.0 + RMS_EPS, RMS_EPS * LN_EPS,
                                     ALU.mult, ALU.add))
                pool.tensor_tensor(rs[2][:, :], ve[2][:, :], minus_half[:, :], ALU.pow).then_inc(S["rstd2"], 1)
                after(pool, "rstd2", n + 1)
                apart(pool)
                pool.tensor_scalar(skip_ab[:, 0:1], rs[2][:, 0:1], 1.0, 1.0, ALU.add, ALU.mult)
                pool.tensor_tensor(skip_ab[:, 1:2], rs[2][:, 0:1], mv[2][:, 0:1], ALU.mult).then_inc(S["skip_ab_ready"], 1)
                o.end()
            elif name in ("K", "Q"):
                k = name.lower()
                o = Order(pool, f"pool{k}_order", 1 if k == "k" else 2, n)
                after(pool, f"{k}_sum", n + 1)
                apart(pool)
                o(pool.tensor_scalar(qk_ms[k][:, :], qk_sum[k][:, :], 1.0 / D, RMS_EPS, ALU.mult, ALU.add))
                root = pool.tensor_tensor(qk_r[k][:, :], qk_ms[k][:, :], minus_half[:, 0:1], ALU.pow)
                if k == "k":
                    root.then_inc(S["k_scale"], 1)
                else:
                    o(root)
                    apart(pool)
                    pool.tensor_scalar(q_neg[:, :], qk_r[k][:, :], -1.0, 1.0, ALU.mult, ALU.mult)\
                        .then_inc(S["q_scale"], 1)
                o.end()

        def whole(eng, item, fori):
            for name in ("res0", "T1", "res1", "res2", "AG1", "LN1a", "TG1", "LN1b", "res3", "res4", "res5",
                         "WB1", "res6", "LN2b", "res7"):
                item(eng, name, -1, 0, -1, 1)
            for t in range(TPC + 1):
                for name, ahead in (("T2", 0), ("T1", 1), ("TE", -1), ("K", 0), ("SK", 1), ("RA", -1), ("LN1a", 1),
                                    ("AG1", 1), ("V", 0), ("TG1", 1), ("LN1b", 1), ("TW", 0), ("RB", -1),
                                    ("WB1", 1), ("Y", -1), ("Q", 0), ("TWV", 0), ("LN2b", 1)):
                    if 0 <= t + ahead < TPC:
                        item(eng, name, -1, t + ahead, -1, 1)
            if item is act_item or item is dve_item:
                for name in ("hi0", "hi1", "hi2", "lo0", "lo1", "lo2"):
                    item(eng, name, -1, TPC - 1, 0, 1)

            def chunk(c, par, **which):
                for name, f, t in chunk_items(**which):
                    item(eng, name, f, t, c, par)

            chunk(0, 0, with1=True, with3=False, first=True)
            chunk(1, 1, with1=True, with3=True)
            with fori(0, (NCH - 4) // 2) as pair:
                chunk(pair * 2 + 2, 0, with1=True, with3=True)
                chunk(pair * 2 + 3, 1, with1=True, with3=True)
            chunk(NCH - 2, 0, with1=True, with3=True)
            chunk(NCH - 1, 1, with1=False, with3=True)
            for name in ("out_a", "out_b"):
                item(eng, name, 0, 0, NCH, 0)
            for t in range(TPC):
                for name in ("LN3a", "LN3b", "T3", "AG3", "TG3", "WB3"):
                    item(eng, name, 0, t, NCH, 0)

        block = ctx.enter_context(nc.Block())

        @block.sync
        def _(sp):
            def item(sp, name, f, t, c, par):
                PAR[0] = 1 - par
                sp_item(sp, name, f, t, c, isinstance(c, int) and c == NCH - 1)

            sp.dma_start(x0[0][:, :], x[0:P, :]).then_inc(x_loaded[0], 16)
            sp.dma_start(const[:, :], consts).then_inc(S["const_loaded"], 16)
            sp.dma_start(bias_raw[:, :], half_bias).then_inc(S["const_loaded"], 16)
            sp.dma_start(gbias[:, :], gate_bias).then_inc(S["const_loaded"], 16)
            sp_load_x(sp, 0, 0)
            for i in range(PIECES):
                after(sp, "res_hi_ready", i - 1)
                after(sp, "res_lo_ready", i - 1)
                sp.dma_start(raw[i % 2][:, 0:PIECE], resident[i]).then_inc(raw_loaded[i % 2], 16)
            for i in range(2):
                after(sp, "res_hi_ready", PIECES - 1 + i)
                after(sp, "res_lo_ready", PIECES - 1 + i)
                sp_load_record(sp, i, i)
            whole(sp, item, sp.Fori)
            for t in range(TPC):
                sp.wait_ge(out_stored[t], 16 * NCH)

        @block.gpsimd
        def _(pool):
            pool.memset(minus_half[:, :], -0.5).then_inc(S["const_ready"], 1)
            pool.wait_ge(S["const_ready"], 1)
            pool.wait_ge(S["bias_ready"], 1)
            pool_rstd(pool, 1, 0)
            whole(pool, pool_item, pool.Fori)

        @block.scalar
        def _(act):
            whole(act, act_item, act.Fori)

        @block.vector
        def _(dve):
            dve.wait_ge(S["const_loaded"], 48)
            dve.tensor_scalar(bias_raw[:, :], bias_raw[:, :], 0.5, None, ALU.mult).then_inc(S["bias_ready"], 1)
            dve.wait_ge(x_loaded[0], 16)
            dve_stats(dve, 1, 0, x0[0][:, :])
            dve_norm(dve, 1, 0, x0[0][:, :])
            whole(dve, dve_item, dve.Fori)

        @block.tensor
        def _(pe):
            pe.wait_ge(S["const_loaded"], 48)
            whole(pe, pe_item, pe.Fori)


def kernel(L0_attn_x, L0_attn_w_qkv, L0_attn_w_swiglu, L0_attn_w_out, L0_ffn_W, L0_ffn_b, L0_ffn_lora_A,
           L0_ffn_lora_B, L0_ffn_gate_w, L0_ffn_gate_b):
    import concourse.bacc as bacc
    from concourse.bass_utils import run_bass_kernel_spmd

    def arr(a):
        return np.asarray(a)

    def by_k(w):
        o, i = w.shape
        return w.T.reshape(i // P, P, o).transpose(1, 0, 2).reshape(P, -1)

    xs = arr(L0_attn_x).reshape(TOKENS, D)
    ag = np.concatenate([arr(L0_ffn_lora_A).reshape(ER, D), arr(L0_ffn_gate_w)], 0)
    lora_b = arr(L0_ffn_lora_B).transpose(0, 2, 1).reshape(ER, D)
    wq, wk, wv = (arr(L0_attn_w_qkv)[i * D:(i + 1) * D] for i in range(3))
    resident = np.concatenate([by_k(ag), lora_b, by_k(arr(L0_ffn_W)), by_k(wk), by_k(wv), by_k(wq)], 1)
    resident = np.ascontiguousarray(resident.reshape(P, PIECES, PIECE).transpose(1, 0, 2))
    up, gate = arr(L0_attn_w_swiglu)[:DFF], arr(L0_attn_w_swiglu)[DFF:]
    w_out = arr(L0_attn_w_out).T
    stream = np.stack([
        np.concatenate([by_k(gate[f * P:(f + 1) * P]), by_k(up[f * P:(f + 1) * P]),
                        w_out[(f - 1) % NF * P:((f - 1) % NF + 1) * P]], 1) for f in range(NF)])
    arrays = {
        "x_rows": np.ascontiguousarray(np.concatenate([xs, xs[:P]], 0)),
        "resident": resident,
        "stream": np.ascontiguousarray(stream),
        "bias": np.ascontiguousarray(np.broadcast_to(arr(L0_ffn_b), (P, D))),
        "gate_bias": np.ascontiguousarray(np.broadcast_to(arr(L0_ffn_gate_b), (P, E))),
        "consts": np.concatenate([np.eye(P, dtype=np.float32), np.ones((P, P), np.float32),
                                  np.tile(np.arange(E, dtype=np.float32), (P, 1))], 1),
    }
    nc = bacc.Bacc("TRN2", target_bir_lowering=False, num_devices=1, dynamic_dma_scratch_size=8192)
    args = [nc.dram_tensor(name, a.shape, F32, kind="ExternalInput").ap() for name, a in arrays.items()]
    out = nc.dram_tensor("out_rows", (TOKENS, D), F32, kind="ExternalOutput").ap()
    build_program(nc, *args, out)
    got = run_bass_kernel_spmd(nc, [arrays], core_ids=[0]).results[0]["out_rows"]
    return got.reshape(L0_attn_x.shape)
```

```python
from contextlib import ExitStack

import numpy as np
import concourse.bass as bass
from concourse import mybir
from concourse.alu_op_type import AluOpType as ALU

F32 = mybir.dt.float32
F32R = mybir.dt.float32r
U32 = mybir.dt.uint32
ACT = mybir.ActivationFunctionType

P = 128
D = 512
KT = D // P
E, R = 8, 16
ER = E * R
AG = ER + E
DFF = 2048
NF = DFF // P
TOKENS = 4096
SEQ = 1024
CHUNK = 512
TPC = CHUNK // P
NCH = TOKENS // CHUNK
CPS = SEQ // CHUNK
LN_EPS = 1e-5
RMS_EPS = 1.1920929e-07
SUM_EPS = 1e-6

O_AG = 0
O_B = O_AG + KT * AG
O_W = O_B + D
O_K = O_W + KT * D
O_V = O_K + KT * D
O_Q = O_V + KT * D
RES = O_Q + KT * D
PIECES = 8
PIECE = RES // PIECES
assert PIECE * PIECES == RES and PIECES % 2 == 0
REC = 2 * D + D
PART = 512

STEPS = (
    "gate act_gate T1 out_a LN3a hi0 hi1 hi2 lo0 lo1 lo2 up act_up AG1 low GT1 out_b SK LN3b",
    "gate act_gate out_a TG1 hi0 hi1 hi2 lo0 lo1 lo2 up act_up low T3 WB1 out_b LN2b AG3 GT3",
    "gate act_gate T2 out_a hi0 hi1 hi2 lo0 lo1 lo2 up act_up low TG3 K V out_b Q LN1a",
    "gate act_gate TW out_a TWV hi0 hi1 hi2 lo0 up act_up TE lo1 lo2 low out_b LN1b RA RB Y WB3 DN3",
)
FIRST_STEP = "out_a T1 out_b hi0 hi1 hi2 lo0 lo1 gate act_gate AG1 GT1 up act_up lo2 low LN3a SK LN3b"
STAGE1 = ("SK", "LN1a", "LN1b", "T1", "AG1", "GT1", "TG1", "WB1", "LN2b", "T2", "K", "V", "Q", "TW", "TWV", "TE",
          "RA", "RB", "Y")
START_STEPS = (("T2", 0), ("T1", 1), ("TE", -1), ("K", 0), ("SK", 1), ("RA", -1), ("LN1a", 1), ("AG1", 1), ("GT1", 1),
               ("V", 0), ("TG1", 1), ("LN1b", 1), ("TW", 0), ("RB", -1), ("WB1", 1), ("Y", -1), ("Q", 0),
               ("LN2b", 1), ("TWV", 0))
LAST_START_STEPS = (("T2", 0), ("T1", 1), ("TE", -1), ("K", 0), ("SK", 1), ("RA", -1), ("LN1a", 1), ("AG1", 1), ("GT1", 1),
                    ("V", 0), ("TG1", 1), ("LN1b", 1), ("TW", 0), ("Q", 0), ("RB", -1), ("Y", -1), ("TWV", 0),
                    ("WB1", 1), ("TE", 0), ("RA", 0), ("RB", 0), ("Y", 0), ("LN2b", 1))
AHEAD = {name for name, ahead in START_STEPS if ahead == 1}
TAIL = range(3, 3 + TPC)
STAGE3 = {piece.format(k): (piece.format(""), k)
          for k in TAIL for piece in ("LN{}a", "LN{}b", "T{}", "AG{}", "GT{}", "TG{}", "WB{}", "DN{}")}
TAIL_STEPS = ("out_a LN3a out_b LN3b LN4a T3 LN4b LN5a T4 LN5b LN6a AG3 GT3 T5 LN6b TG3 T6 AG4 GT4 AG5 GT5 WB3 "
              "TG4 AG6 GT6 DN3 WB4 TG5 WB5 DN4 TG6 WB6 DN5 DN6")


def chunk_items(with1, with3, first=False):
    for f in range(NF):
        for name in (STEPS[f % TPC] if f else FIRST_STEP).split():
            if name in STAGE1 and not with1 and not (name == "SK" and f == 0):
                continue
            if first and f < TPC and name in AHEAD:
                continue
            if name in STAGE3 and not with3 or first and f == 0 and name in ("out_a", "out_b"):
                continue
            yield name, f, f // TPC


def build_program(nc, x, resident, stream, bias, gate_bias, consts, out):
    with ExitStack() as ctx:
        def sb(name, shape, dt=F32):
            return ctx.enter_context(nc.sbuf_tensor(name, shape, dt))

        def bank(name):
            return ctx.enter_context(nc.psum_tensor(name, [P, 512], F32))

        def sem(name):
            return ctx.enter_context(nc.semaphore(name))

        res = sb("res", [P, 2, RES], F32R)
        res_hi, res_lo = res[:, 0, :], res[:, 1, :]
        raw = [sb(f"raw{i}", [P, REC]) for i in range(2)]
        rec_hi = [sb(f"rec_hi{i}", [P, REC], F32R) for i in range(2)]
        rec_lo = [sb(f"rec_lo{i}", [P, REC], F32R) for i in range(2)]
        half_bias = sb("half_bias", [P, D])
        gbias = sb("gbias", [P, E])
        const = sb("const", [P, 2 * P + E])
        ident, ones, iota = const[:, 0:P], const[:, P:2 * P], const[:, 2 * P:2 * P + E]
        minus_half = sb("minus_half", [P, 2])
        x0 = [sb(f"x0_{i}", [P, D]) for i in range(2)]
        x1 = sb("x1", [P, D])
        skip = [[sb(f"skip{p}_{t}", [P, D]) for t in range(TPC)] for p in range(2)]
        y_hi = [sb(f"y_hi{p}", [P, KT, CHUNK], F32R) for p in range(2)]
        y_lo = [sb(f"y_lo{p}", [P, KT, CHUNK], F32R) for p in range(2)]
        w_tok, wv_tok, eq_tok = sb("w_tok", [P, D]), sb("wv_tok", [P, D]), sb("eq_tok", [P, D])
        cum_w, cum_wv, yf = sb("cum_w", [P, D]), sb("cum_wv", [P, D]), sb("yf", [P, D])
        carry_w, carry_wv = sb("carry_w", [P, KT]), sb("carry_wv", [P, KT])
        hid = sb("hid", [P, CHUNK])
        h_hi = [sb(f"h_hi{i}", [P, CHUNK], F32R) for i in range(2)]
        h_lo = [sb(f"h_lo{i}", [P, CHUNK], F32R) for i in range(2)]
        norm = {k: sb(f"norm{k}", [P, D]) for k in (1, 2, 3)}
        xt_hi = {k: sb(f"xt_hi{k}", [P, D], F32R) for k in (1, 2, 3)}
        xt_lo = {k: sb(f"xt_lo{k}", [P, D], F32R) for k in (1, 2, 3)}
        bn6 = {k: sb(f"bn6_{k}", [P, 6]) for k in (1, 2, *TAIL)}
        mv = {k: sb(f"mv{k}", [P, 2]) for k in (1, 2, *TAIL)}
        ve = {k: sb(f"ve{k}", [P, 2]) for k in (1, 2, *TAIL)}
        rs = {k: sb(f"rs{k}", [P, 2]) for k in (1, 2, *TAIL)}
        skip_ab = sb("skip_ab", [P, 2])
        lg = {k: sb(f"lg{k}", [P, E]) for k in (1, *TAIL)}
        top = {k: sb(f"top{k}", [P, 8]) for k in (1, *TAIL)}
        idx = {k: sb(f"idx{k}", [P, 8], U32) for k in (1, *TAIL)}
        idxf = {k: sb(f"idxf{k}", [P, 2]) for k in (1, *TAIL)}
        ex = {k: sb(f"ex{k}", [P, 1]) for k in (1, *TAIL)}
        gden = {k: sb(f"gden{k}", [P, 1]) for k in (1, *TAIL)}
        grec = {k: sb(f"grec{k}", [P, 1]) for k in (1, *TAIL)}
        second = {k: sb(f"second{k}", [P, E]) for k in (1, *TAIL)}
        gt = {k: sb(f"gt{k}", [P, E]) for k in (1, *TAIL)}
        gated = {k: sb(f"gated{k}", [P, ER]) for k in (1, 3)}
        gt_hi = {k: sb(f"gt_hi{k}", [P, P], F32R) for k in (1, 3)}
        gt_lo = {k: sb(f"gt_lo{k}", [P, P], F32R) for k in (1, 3)}
        for k, rows, at in ((4, norm[1], 0), (5, norm[2], 1), (6, w_tok, 2)):
            norm[k] = rows
            xt_hi[k], xt_lo[k] = y_hi[0][:, at, :], y_lo[0][:, at, :]
            gated[k] = (wv_tok, eq_tok, yf)[at][:, 0:ER]
            gt_hi[k], gt_lo[k] = y_hi[0][:, 3, at * P:(at + 1) * P], y_lo[0][:, 3, at * P:(at + 1) * P]
        qk_sum = {k: sb(f"{k}_sum", [P, 1]) for k in "kq"}
        qk_ms = {k: sb(f"{k}_ms", [P, 1]) for k in "kq"}
        qk_r = {k: sb(f"{k}_r", [P, 1]) for k in "kq"}
        q_neg = sb("q_neg", [P, 1])

        bank_g, bank_u = bank("bank_g"), bank("bank_u")
        bank_o = [bank(f"bank_o{t}") for t in range(TPC)]
        side_a, side_b = bank("side_a"), bank("side_b")
        BANK = {"T1": side_a, "AG1": side_a, "TG1": side_a, "WB1": side_a, "T2": side_a, "K": side_a, "V": side_b,
                "Q": side_a, "TW": side_b, "TWV": side_a, "TE": side_b}
        for name, (_, k) in STAGE3.items():
            BANK[name] = (side_b, side_a, bank_g, bank_u)[k - 3]
        EARLY = dict(BANK, T1=bank_o[0], AG1=bank_o[1], TG1=bank_o[2], WB1=bank_o[3], T2=bank_g, K=bank_u,
                     TW=bank_g, TWV=bank_u)

        def side_bank(name, f):
            return (EARLY if f < 0 else BANK)[name]

        S = {}
        for name in (
            "const_loaded", "bias_ready", "const_ready", "res_hi_ready", "res_lo_ready",
            "rec_hi_ready", "rec_lo_ready",
            *(f"{event}{k}" for k in (1, 2, *TAIL) for event in ("stats", "rstd", "norm", "xt_hi", "xt_lo")),
            *(f"t{k}_done" for k in (1, 2, *TAIL)),
            *(f"{event}{k}" for k in (1, *TAIL) for event in ("top", "ex", "gated", "gt_hi", "gt_lo")),
            *(f"{piece}{k}_done" for k in (1, *TAIL) for piece in ("ag", "tg", "wb")),
            "resid1", "resid3", "skip_ab_ready", "skip_ready", "x1_ready", "x3_ready",
            "k_done", "k_sum", "k_scale", "w_ready", "v_done", "wv_ready", "q_done", "q_sum", "q_scale",
            "eq_ready", "tw_done", "twv_done", "te_done", "cumw_ready", "cumwv_ready", "den_ready",
            "yf_ready", "yhi_ready", "ylo_ready",
            "g_done", "u_done", "tanh_ready", "gate_used", "h_ready", "hhi_ready", "hlo_ready", "out_done",
            "x2_ready",
            *(f"ln{k}_order" for k in (1, 2, *TAIL)), *(f"gate{k}_order" for k in (1, *TAIL)),
            "sum_order", "y_order",
            *(f"pool{k}_order" for k in (1, 2, *TAIL)), "poolk_order", "poolq_order",
        ):
            S[name] = sem(name)
        raw_loaded = [sem("raw0_loaded"), sem("raw1_loaded")]
        x_loaded = [sem("x0_loaded"), sem("x1_loaded")]
        out_stored = [sem(f"out_stored{t}") for t in range(TPC)]

        def after(eng, name, count):
            if not (isinstance(count, int) and count <= 0):
                eng.wait_ge(S[name], count)

        def apart(eng):
            eng.nop(nofuse=True)

        class Order:

            def __init__(self, eng, name, per, n):
                self.eng, self.sem, self.per, self.n, self.done = eng, S[name], per, n, 0

            def __call__(self, ins):
                ins.then_inc(self.sem, 1)
                self.done += 1
                assert self.done <= self.per
                self.eng.wait_ge(self.sem, self.n * self.per + self.done)

            def end(self):
                assert self.done == self.per, (self.done, self.per)

        def y_half(par, t, half):
            kts, toks = slice(half * KT // 2, (half + 1) * KT // 2), slice(t * P, (t + 1) * P)
            return (y_hi[par][:, kts, toks], yf[:, :].rearrange("p (k m) -> p k m", k=KT)[:, kts, :],
                    y_lo[par][:, kts, toks])

        def f32(ap):
            return ap.bitcast(F32)

        def sp_load_record(sp, f, ring):
            sp.dma_start(raw[ring][:, :], stream[f % NF]).then_inc(raw_loaded[ring], 16)

        def sp_item(sp, name, f, t, c, par):
            j, m = c + 1, 4 * (c - 1) + t
            last = isinstance(c, int) and c == NCH - 1
            if name == "gate" and not (last and f == NF - 1):
                after(sp, "rec_hi_ready", 3 * (NF * c + f + 1))
                after(sp, "rec_lo_ready", 3 * (NF * c + f + 1))
                sp_load_record(sp, f + 2, f % 2)
            elif name == "T1" and not (f < 0 and t < 2):
                sp_load_x(sp, 4 * j + t, t)
            elif name in STAGE3 and STAGE3[name][0] == "DN":
                after(sp, "x3_ready", m + 1)
                sp.dma_start(out[bass.ds(m * P, P), :], skip[1 - par][t][:, :]).then_inc(out_stored[t], 16)

        def sp_load_x(sp, n, t):
            after(sp, "x1_ready", n)
            sp.dma_start(x0[(t + 1) % 2][:, :], x[bass.ds((n + 1) * P, P), :]).then_inc(x_loaded[(t + 1) % 2], 16)

        def mm3(pe, acc, st_hi, st_lo, mv_hi, mv_lo, start, stop):
            pe.matmul(acc, st_hi, mv_hi, start=start, stop=False)
            pe.matmul(acc, st_hi, mv_lo, start=False, stop=False)
            return pe.matmul(acc, st_lo, mv_hi, start=False, stop=stop)

        def pe_transpose4(pe, b, src):
            for kt in range(KT):
                last = pe.transpose(b[:, kt * P:(kt + 1) * P], src[:, kt * P:(kt + 1) * P], ident)
            return last

        def pe_from_x(pe, k, acc, o, width, stop=True):
            for kt in range(KT):
                a, b = o + kt * width, o + (kt + 1) * width
                cols = slice(kt * P, (kt + 1) * P)
                last = mm3(pe, acc, xt_hi[k][:, cols], xt_lo[k][:, cols], res_hi[:, a:b], res_lo[:, a:b],
                           kt == 0, stop and kt == KT - 1)
            return last

        def pe_lora_a(pe, k, b):
            for kt in range(KT):
                w, cols = slice(O_AG + kt * AG, O_AG + (kt + 1) * AG), slice(kt * P, (kt + 1) * P)
                if kt == KT - 1:
                    pe.matmul(b[:, 0:AG], xt_lo[k][:, cols], res_hi[:, w], start=False, stop=False)
                last = pe.matmul(b[:, 0:2 * AG].rearrange("p (h a) -> p h a", h=2), xt_hi[k][:, cols], res[:, :, w],
                                 start=kt == 0, stop=kt == KT - 1)
                if kt < KT - 1:
                    pe.matmul(b[:, 0:AG], xt_lo[k][:, cols], res_hi[:, w], start=False, stop=False)
            return last

        def res_need(end):
            return -(-end // PIECE)

        def pe_item(pe, name, f, t, c, par):
            n, m, F = 4 * (c + 1) + t, 4 * (c - 1) + t, NF * c + f
            ring = f % 2
            if name == "gate":
                if f == 0:
                    after(pe, "ylo_ready", 2 * TPC * (c + 1) - 1)
                after(pe, "rec_lo_ready", 3 * F + 1)
                after(pe, "gate_used", F)
                for kt in range(KT):
                    if f == 0 and kt == KT // 2:
                        after(pe, "ylo_ready", 2 * TPC * (c + 1))
                    cols = slice(kt * P, (kt + 1) * P)
                    last = mm3(pe, bank_g[:, :], rec_hi[ring][:, cols], rec_lo[ring][:, cols],
                               y_hi[par][:, kt, :], y_lo[par][:, kt, :], kt == 0, kt == KT - 1)
                last.then_inc(S["g_done"], 1)
            elif name == "up":
                after(pe, "rec_lo_ready", 3 * F + 2)
                after(pe, "h_ready", F)
                for kt in range(KT):
                    cols = slice(D + kt * P, D + (kt + 1) * P)
                    last = mm3(pe, bank_u[:, :], rec_hi[ring][:, cols], rec_lo[ring][:, cols],
                               y_hi[par][:, kt, :], y_lo[par][:, kt, :], kt == 0, kt == KT - 1)
                last.then_inc(S["u_done"], 1)
            elif name in ("out_a", "out_b"):
                if name == "out_a":
                    after(pe, "rec_lo_ready", 3 * F + 3)
                    after(pe, "hlo_ready", F)
                    if f == 1:
                        after(pe, "x2_ready", 4 * c)
                for t2 in ((0, 1) if name == "out_a" else (2, 3)):
                    cols = slice(t2 * P, (t2 + 1) * P)
                    last = mm3(pe, bank_o[t2][:, :], h_hi[1 - ring][:, cols], h_lo[1 - ring][:, cols],
                               rec_hi[ring][:, 2 * D:REC], rec_lo[ring][:, 2 * D:REC], f == 1, f == 0)
                last.then_inc(S["out_done"], 1)
            elif name in STAGE1:
                pe_stage1(pe, name, n, m, f)
            elif name in STAGE3:
                pe_stage3(pe, *STAGE3[name], n, m)

        def pe_stage1(pe, name, n, m, f):
            if name not in BANK:
                return
            b = side_bank(name, f)
            if name == "T1":
                if f >= 0:
                    after(pe, "cumwv_ready", n)
                after(pe, "norm1", n + 1)
                pe_transpose4(pe, b, norm[1]).then_inc(S["t1_done"], 1)
            elif name == "AG1":
                pe.wait_ge(S["res_lo_ready"], res_need(O_B))
                after(pe, "xt_lo1", n + 1)
                pe_lora_a(pe, 1, b).then_inc(S["ag1_done"], 1)
            elif name == "TG1":
                after(pe, "gated1", n + 1)
                pe.transpose(b[:, 0:P], gated[1][:, :], ident).then_inc(S["tg1_done"], 1)
            elif name == "WB1":
                pe.wait_ge(S["res_lo_ready"], res_need(O_K))
                after(pe, "gt_lo1", n + 1)
                pe_from_x(pe, 1, b[:, :], O_W, D, stop=False)
                mm3(pe, b[:, :], gt_hi[1][:, :], gt_lo[1][:, :], res_hi[:, O_B:O_W], res_lo[:, O_B:O_W],
                    False, True).then_inc(S["wb1_done"], 1)
            elif name == "T2":
                after(pe, "norm2", n + 1)
                pe_transpose4(pe, b, norm[2]).then_inc(S["t2_done"], 1)
            elif name == "K":
                pe.wait_ge(S["res_lo_ready"], res_need(O_V))
                after(pe, "xt_lo2", n + 1)
                after(pe, "cumwv_ready", n)
                pe_from_x(pe, 2, b[:, :], O_K, D).then_inc(S["k_done"], 1)
            elif name == "V":
                pe.wait_ge(S["res_lo_ready"], res_need(O_Q))
                after(pe, "den_ready", n)
                if not (isinstance(m, int) and m < 0):
                    after(pe, "gt_lo3", m + 1)
                pe_from_x(pe, 2, b[:, :], O_V, D).then_inc(S["v_done"], 1)
            elif name == "Q":
                pe.wait_ge(S["res_lo_ready"], PIECES)
                after(pe, "w_ready", n + 1)
                pe_from_x(pe, 2, b[:, :], O_Q, D).then_inc(S["q_done"], 1)
            elif name == "TW":
                after(pe, "w_ready", n + 1)
                if f >= 0:
                    after(pe, "wv_ready", n + 1)
                pe_transpose4(pe, b, w_tok).then_inc(S["tw_done"], 1)
            elif name == "TWV":
                after(pe, "wv_ready", n + 1)
                if f >= 0:
                    after(pe, "eq_ready", n + 1)
                pe_transpose4(pe, b, wv_tok).then_inc(S["twv_done"], 1)
            elif name == "TE":
                after(pe, "eq_ready", n + 1)
                after(pe, "cumw_ready", n + 1)
                pe_transpose4(pe, b, eq_tok).then_inc(S["te_done"], 1)

        def set_count(k, m):
            return m if k == 3 else 0

        def pe_stage3(pe, piece, k, n, m):
            if piece in ("LNa", "LNb"):
                return
            b, i = BANK[f"T{k}"], set_count(k, m)
            if piece == "T":
                if k == 3:
                    after(pe, "den_ready", min(n, TPC * NCH) if isinstance(n, int) else n)
                    after(pe, "x3_ready", m)
                after(pe, f"norm{k}", i + 1)
                pe_transpose4(pe, b, norm[k]).then_inc(S[f"t{k}_done"], 1)
            elif piece == "AG":
                after(pe, f"xt_lo{k}", i + 1)
                pe_lora_a(pe, k, b).then_inc(S[f"ag{k}_done"], 1)
            elif piece == "TG":
                after(pe, f"gated{k}", i + 1)
                pe.transpose(b[:, 0:P], gated[k][:, :], ident).then_inc(S[f"tg{k}_done"], 1)
            elif piece == "WB":
                if not (isinstance(n, int) and n >= TPC * NCH):
                    after(pe, "den_ready", n + 1)
                after(pe, f"gt_lo{k}", i + 1)
                pe_from_x(pe, k, b[:, :], O_W, D, stop=False)
                mm3(pe, b[:, :], gt_hi[k][:, :], gt_lo[k][:, :], res_hi[:, O_B:O_W], res_lo[:, O_B:O_W],
                    False, True).then_inc(S[f"wb{k}_done"], 1)

        def act_item(act, name, f, t, c, par):
            n, m, F = 4 * (c + 1) + t, 4 * (c - 1) + t, NF * c + f
            ring = f % 2
            if name == "gate":
                after(act, "g_done", F + 1)
                after(act, "hlo_ready", F)
                act.activation(hid[:, :], bank_g[:, :], ACT.Tanh, scale=0.5).then_inc(S["tanh_ready"], 1)
            elif name == "act_up":
                after(act, "h_ready", F + 1)
                after(act, "out_done", 2 * (F - 1))
                act.activation(h_hi[ring][:, :], hid[:, :], ACT.Copy).then_inc(S["hhi_ready"], 1)
            elif name in ("hi0", "hi1", "hi2"):
                split_hi(act, int(name[-1]), 1 - ring, f + 1, F + 1, c)
            elif name in STAGE1:
                act_stage1(act, name, n, t, c, 1 - par, f)
            elif name in STAGE3:
                k = STAGE3[name][1]
                act_ffn(act, name, k, set_count(k, m), f)
            elif name.startswith("res"):
                i = int(name[3:])
                cols = slice(i * PIECE, (i + 1) * PIECE)
                act.wait_ge(raw_loaded[i % 2], 16 * (i // 2 + 1))
                act.activation(res_hi[:, cols], raw[i % 2][:, 0:PIECE], ACT.Copy).then_inc(S["res_hi_ready"], 1)

        def split_wait_ring(eng, part, F):
            if part == 0:
                after(eng, "g_done", F - 1)
            elif part == 1:
                after(eng, "u_done", F - 1)
            else:
                after(eng, "out_done", 2 * (F - 2))

        def raw_count(f, c):
            return 16 * (PIECES // 2 + NF // 2 * c + f // 2 + 1)

        def split_hi(act, part, ring, f, F, c):
            cols = slice(part * PART, (part + 1) * PART)
            if part == 0:
                act.wait_ge(raw_loaded[ring], raw_count(f, c))
            split_wait_ring(act, part, F)
            act.activation(rec_hi[ring][:, cols], raw[ring][:, cols], ACT.Copy).then_inc(S["rec_hi_ready"], 1)

        def act_ffn(act, name, k, n, f):
            if name == f"T{k}":
                after(act, f"t{k}_done", n + 1)
                after(act, f"wb{k}_done", n)
                act.activation(xt_hi[k][:, :], side_bank(name, f)[:, :], ACT.Copy).then_inc(S[f"xt_hi{k}"], 1)
            elif name == f"AG{k}":
                after(act, f"top{k}", n + 1)
                act.activation(ex[k][:, :], top[k][:, 0:1], ACT.Exp, bias=top[k][:, 1:2],
                               scale=-1.0).then_inc(S[f"ex{k}"], 1)
            elif name == f"TG{k}":
                after(act, f"tg{k}_done", n + 1)
                act.activation(gt_hi[k][:, :], side_bank(name, f)[:, 0:P], ACT.Copy).then_inc(S[f"gt_hi{k}"], 1)

        def act_stage1(act, name, n, t, c, par, f):
            act_ffn(act, name, 1, n, f)
            if name == "T2":
                after(act, "t2_done", n + 1)
                after(act, "q_done", n)
                act.activation(xt_hi[2][:, :], side_bank(name, f)[:, :], ACT.Copy).then_inc(S["xt_hi2"], 1)
            elif name in ("K", "Q"):
                k = name.lower()
                dst, gone, ready, sign = ((w_tok, "tw_done", "w_ready", 1) if k == "k" else
                                          (eq_tok, "te_done", "eq_ready", -1))
                after(act, f"{k}_done", n + 1)
                after(act, gone, n)
                act.activation(dst[:, :], side_bank(name, f)[:, :], ACT.Square,
                               accum_out=qk_sum[k][:, :]).then_inc(S[f"{k}_sum"], 1)
                after(act, f"{k}_scale", n + 1)
                act.activation(dst[:, :], side_bank(name, f)[:, :], ACT.Exp,
                               scale=(qk_r["k"] if sign > 0 else q_neg)[:, 0:1]).then_inc(S[ready], 1)
            elif name in ("RA", "RB"):
                half = "RA RB".split().index(name)
                after(act, "yf_ready", 2 * n + half + 1)
                if half == 0:
                    after(act, "u_done", NF * c)
                dst, src, _ = y_half(par, t, half)
                act.activation(dst, src, ACT.Copy).then_inc(S["yhi_ready"], 1)

        def dve_item(dve, name, f, t, c, par):
            n, m, F = 4 * (c + 1) + t, 4 * (c - 1) + t, NF * c + f
            ring = f % 2
            if name == "act_gate":
                after(dve, "tanh_ready", F + 1)
                o = Order(dve, "gate_used", 1, F)
                o(dve.scalar_tensor_tensor(out=hid[:, :], in0=hid[:, :], scalar=1.0, in1=bank_g[:, :],
                                           op0=ALU.add, op1=ALU.mult))
                o.end()
            elif name == "act_up":
                after(dve, "u_done", F + 1)
                dve.tensor_tensor(hid[:, :], hid[:, :], bank_u[:, :], ALU.mult).then_inc(S["h_ready"], 1)
            elif name == "low":
                after(dve, "hhi_ready", F + 1)
                dve.tensor_tensor(h_lo[ring][:, :], hid[:, :], f32(h_hi[ring][:, :]),
                                  ALU.subtract).then_inc(S["hlo_ready"], 1)
            elif name in ("out_a", "out_b"):
                if f == 0:
                    after(dve, "out_done", 2 * F - (1 if name == "out_a" else 0))
                    after(dve, "skip_ready", NF // 4 * c)
                    for t2 in ((0, 1) if name == "out_a" else (2, 3)):
                        sk = skip[1 - par][t2]
                        dve.scalar_tensor_tensor(out=sk[:, :], in0=bank_o[t2][:, :], scalar=0.5, in1=sk[:, :],
                                                 op0=ALU.mult, op1=ALU.add).then_inc(S["x2_ready"], 1)
            elif name in ("lo0", "lo1", "lo2"):
                split_lo(dve, int(name[-1]), 1 - ring, F + 1)
            elif name in STAGE1:
                dve_stage1(dve, name, n, t, c, 1 - par, f)
            elif name in STAGE3:
                dve_stage3(dve, name, *STAGE3[name], m, t, 1 - par, f)
            elif name.startswith("res"):
                i = int(name[3:])
                cols = slice(i * PIECE, (i + 1) * PIECE)
                after(dve, "res_hi_ready", i + 1)
                dve.tensor_tensor(res_lo[:, cols], raw[i % 2][:, 0:PIECE], f32(res_hi[:, cols]),
                                  ALU.subtract).then_inc(S["res_lo_ready"], 1)

        def split_lo(dve, part, ring, F):
            cols = slice(part * PART, (part + 1) * PART)
            after(dve, "rec_hi_ready", 3 * F + part + 1)
            split_wait_ring(dve, part, F)
            dve.tensor_tensor(rec_lo[ring][:, cols], raw[ring][:, cols], f32(rec_hi[ring][:, cols]),
                              ALU.subtract).then_inc(S["rec_lo_ready"], 1)

        def dve_ffn(dve, name, k, n, f):
            if name == f"T{k}":
                after(dve, f"xt_hi{k}", n + 1)
                dve.tensor_tensor(xt_lo[k][:, :], side_bank(name, f)[:, :], f32(xt_hi[k][:, :]),
                                  ALU.subtract).then_inc(S[f"xt_lo{k}"], 1)
            elif name == f"AG{k}":
                dve_choice(dve, k, n, side_bank(name, f))
            elif name == f"GT{k}":
                dve_gating(dve, k, n)
            elif name == f"TG{k}":
                after(dve, f"gt_hi{k}", n + 1)
                dve.tensor_tensor(gt_lo[k][:, :], side_bank(name, f)[:, 0:P], f32(gt_hi[k][:, :]),
                                  ALU.subtract).then_inc(S[f"gt_lo{k}"], 1)

        def dve_choice(dve, k, n, b):
            order, base = S[f"gate{k}_order"], 10 * n
            after(dve, f"ag{k}_done", n + 1)
            dve.tensor_tensor(lg[k][:, :], b[:, ER:AG], gbias[:, :], ALU.add).then_inc(order, 1)
            after(dve, f"tg{k}_done", n)
            dve.tensor_copy(gated[k][:, :], b[:, AG:AG + ER]).then_inc(order, 1)
            dve.wait_ge(order, base + 1)
            dve.tensor_tensor(lg[k][:, :], lg[k][:, :], b[:, AG + ER:2 * AG], ALU.add).then_inc(order, 1)
            dve.wait_ge(order, base + 3)
            apart(dve)
            dve.max(top[k][:, :], lg[k][:, :]).then_inc(S[f"top{k}"], 1)
            after(dve, f"top{k}", n + 1)
            apart(dve)
            dve.max_index(idx[k][:, :], top[k][:, :], lg[k][:, :]).then_inc(order, 1)
            dve.tensor_tensor(gated[k][:, :], b[:, 0:ER], gated[k][:, :], ALU.add).then_inc(order, 1)

        def dve_gating(dve, k, n):
            order, base = S[f"gate{k}_order"], 10 * n
            dve.wait_ge(order, base + 4)
            dve.tensor_copy(idxf[k][:, :], idx[k][:, 0:2]).then_inc(order, 1)
            after(dve, f"ex{k}", n + 1)
            dve.tensor_scalar(gden[k][:, :], ex[k][:, :], 1.0, None, ALU.add).then_inc(order, 1)
            dve.wait_ge(order, base + 6)
            dve.tensor_scalar(second[k][:, :], iota, idxf[k][:, 1:2], ex[k][:, :],
                              ALU.is_equal, ALU.mult).then_inc(order, 1)
            dve.wait_ge(order, base + 7)
            dve.reciprocal(grec[k][:, :], gden[k][:, :]).then_inc(order, 1)
            dve.wait_ge(order, base + 8)
            dve.scalar_tensor_tensor(out=gt[k][:, :], in0=iota, scalar=idxf[k][:, 0:1], in1=second[k][:, :],
                                     op0=ALU.is_equal, op1=ALU.add).then_inc(order, 1)
            dve.wait_ge(order, base + 10)
            dve.scalar_tensor_tensor(out=gated[k][:, :].rearrange("p (e r) -> p e r", e=E),
                                     in0=gated[k][:, :].rearrange("p (e r) -> p e r", e=E), scalar=grec[k][:, 0:1],
                                     in1=gt[k][:, :].unsqueeze(2).to_broadcast([P, E, R]),
                                     op0=ALU.mult, op1=ALU.mult).then_inc(S[f"gated{k}"], 1)

        def dve_stats(dve, k, n, src):
            o = Order(dve, f"ln{k}_order", 1, n)
            o(dve.bn_stats(bn6[k][:, :], src))
            apart(dve)
            dve.bn_aggr(mv[k][:, :], bn6[k][:, :]).then_inc(S[f"stats{k}"], 1)

        def dve_norm(dve, k, n, src):
            after(dve, f"rstd{k}", n + 1)
            after(dve, f"t{k}_done", n)
            col = 1 if k == 2 else 0
            dve.tensor_scalar(norm[k][:, :], src, mv[k][:, 0:1], rs[k][:, col:col + 1],
                              ALU.subtract, ALU.mult).then_inc(S[f"norm{k}"], 1)

        def x_count(n, t):
            return 8 * (n - t % 2) + 16

        def dve_stage1(dve, name, n, t, c, par, f):
            j = c + 1
            x_next = x0[(t + 1) % 2][:, :]
            dve_ffn(dve, name, 1, n, f)
            if name == "LN1a":
                dve.wait_ge(x_loaded[(t + 1) % 2], x_count(n + 1, t + 1))
                dve_stats(dve, 1, n + 1, x_next)
            elif name == "LN1b":
                dve_norm(dve, 1, n + 1, x_next)
            if name == "WB1":
                after(dve, "wb1_done", n + 1)
                after(dve, "resid1", n + 1)
                dve.scalar_tensor_tensor(out=x1[:, :], in0=side_bank(name, f)[:, :], scalar=0.5, in1=x0[t % 2][:, :],
                                         op0=ALU.mult, op1=ALU.add).then_inc(S["x1_ready"], 1)
                after(dve, "x1_ready", n + 1)
                dve_stats(dve, 2, n, x1[:, :])
            elif name == "LN2b":
                dve_norm(dve, 2, n, x1[:, :])
            elif name == "SK":
                chunk, par_s, t_s = (j, par, t - 1) if t else (c, 1 - par, TPC - 1)
                if not (isinstance(chunk, int) and chunk < 2):
                    dve.wait_ge(out_stored[t_s], 16 * (chunk - 1))
                after(dve, "skip_ab_ready", n)
                apart(dve)
                dve.tensor_scalar(skip[par_s][t_s][:, :], x1[:, :], skip_ab[:, 0:1], skip_ab[:, 1:2],
                                  ALU.mult, ALU.subtract).then_inc(S["skip_ready"], 1)
            elif name == "T2":
                after(dve, "xt_hi2", n + 1)
                dve.tensor_tensor(xt_lo[2][:, :], side_bank(name, f)[:, :], f32(xt_hi[2][:, :]),
                                  ALU.subtract).then_inc(S["xt_lo2"], 1)
            elif name == "V":
                after(dve, "v_done", n + 1)
                after(dve, "w_ready", n + 1)
                after(dve, "twv_done", n)
                dve.tensor_tensor(wv_tok[:, :], w_tok[:, :], side_bank(name, f)[:, :], ALU.mult).then_inc(S["wv_ready"], 1)
            elif name == "TW":
                after(dve, "tw_done", n + 1)
                dve_scan(dve, n, 0, cum_w, carry_w, side_bank(name, f), SUM_EPS, t == 0 and par % CPS == 0, "cumw_ready")
            elif name == "TWV":
                after(dve, "twv_done", n + 1)
                dve_scan(dve, n, 1, cum_wv, carry_wv, side_bank(name, f), 0.0, t == 0 and par % CPS == 0,
                         "cumwv_ready")
            elif name == "TE":
                after(dve, "te_done", n + 1)
                dve.scalar_tensor_tensor(out=yf[:, :], in0=side_bank(name, f)[:, :], scalar=1.0, in1=cum_w[:, :],
                                         op0=ALU.add, op1=ALU.mult).then_inc(S["den_ready"], 1)
            elif name == "RA":
                after(dve, "den_ready", n + 1)
                dve_y(dve, n, 0)
            elif name == "RB":
                dve_y(dve, n, 1)
            elif name == "Y":
                for half in range(2):
                    after(dve, "yhi_ready", 2 * n + half + 1)
                    hi, src, lo = y_half(par, t, half)
                    dve.tensor_tensor(lo, src, f32(hi), ALU.subtract).then_inc(S["ylo_ready"], 1)

        def dve_y(dve, n, half):
            cols = slice(half * D // 2, (half + 1) * D // 2)
            dve.reciprocal(yf[:, cols], yf[:, cols]).then_inc(S["y_order"], 1)
            dve.wait_ge(S["y_order"], 2 * n + half + 1)
            dve.tensor_tensor(yf[:, cols], yf[:, cols], cum_wv[:, cols], ALU.mult).then_inc(S["yf_ready"], 1)

        def dve_scan(dve, n, which, cum, carry, b, start, fresh, ready):
            for kt in range(KT):
                cols = slice(kt * P, (kt + 1) * P)
                last = dve.tensor_tensor_scan(cum[:, cols], ones, b[:, cols],
                                              start if fresh else carry[:, kt:kt + 1], ALU.mult, ALU.add)
            last.then_inc(S[ready], 1)
            dve.wait_ge(S[ready], n + 1)
            dve.tensor_copy(carry[:, :].unsqueeze(2),
                            cum[:, :].rearrange("p (k m) -> p k m", k=KT)[:, :, P - 1:P]).then_inc(S["sum_order"], 1)
            dve.wait_ge(S["sum_order"], 2 * n + which + 1)

        def dve_stage3(dve, name, piece, k, m, t, par, f):
            sk, i = skip[par][t], set_count(k, m)
            if piece == "LNa":
                after(dve, "x2_ready", m + 1)
                dve_stats(dve, k, i, sk[:, :])
            elif piece == "LNb":
                dve_norm(dve, k, i, sk[:, :])
            dve_ffn(dve, name, k, i, f)
            if piece == "DN":
                after(dve, f"wb{k}_done", i + 1)
                after(dve, "resid3", m + 1)
                dve.scalar_tensor_tensor(out=sk[:, :], in0=BANK[name][:, :], scalar=0.5, in1=sk[:, :],
                                         op0=ALU.mult, op1=ALU.add).then_inc(S["x3_ready"], 1)

        def pool_item(pool, name, f, t, c, par):
            n, m = 4 * (c + 1) + t, 4 * (c - 1) + t
            if name in STAGE1:
                pool_stage1(pool, name, n, t)
            elif name in STAGE3 and STAGE3[name][0] == "LNa":
                k = STAGE3[name][1]
                pool_rstd(pool, k, set_count(k, m))
            elif name in STAGE3 and STAGE3[name][0] == "T":
                k = STAGE3[name][1]
                after(pool, f"norm{k}", set_count(k, m) + 1)
                sk = skip[1 - par][t]
                pool.tensor_tensor(sk[:, :], sk[:, :], half_bias[:, :], ALU.add).then_inc(S["resid3"], 1)

        def pool_rstd(pool, k, n):
            o = Order(pool, f"pool{k}_order", 1, n)
            after(pool, f"stats{k}", n + 1)
            apart(pool)
            o(pool.tensor_scalar(ve[k][:, 0:1], mv[k][:, 1:2], LN_EPS, 1.0, ALU.add, ALU.mult))
            pool.tensor_tensor(rs[k][:, 0:1], ve[k][:, 0:1], minus_half[:, 0:1], ALU.pow).then_inc(S[f"rstd{k}"], 1)

        def pool_stage1(pool, name, n, t):
            if name == "LN1a":
                pool_rstd(pool, 1, n + 1)
            elif name == "T1":
                after(pool, "norm1", n + 1)
                x = x0[t % 2]
                pool.tensor_tensor(x[:, :], x[:, :], half_bias[:, :], ALU.add).then_inc(S["resid1"], 1)
            elif name == "WB1":
                o = Order(pool, "pool2_order", 1, n)
                after(pool, "stats2", n + 1)
                apart(pool)
                pool.tensor_scalar(ve[2][:, 0:1], mv[2][:, 1:2], LN_EPS, 1.0, ALU.add, ALU.mult)
                apart(pool)
                o(pool.tensor_scalar(ve[2][:, 1:2], mv[2][:, 1:2], 1.0 + RMS_EPS, RMS_EPS * LN_EPS,
                                     ALU.mult, ALU.add))
                pool.tensor_tensor(rs[2][:, :], ve[2][:, :], minus_half[:, :], ALU.pow).then_inc(S["rstd2"], 1)
                after(pool, "rstd2", n + 1)
                apart(pool)
                pool.tensor_scalar(skip_ab[:, 0:1], rs[2][:, 0:1], 1.0, 1.0, ALU.add, ALU.mult)
                pool.tensor_tensor(skip_ab[:, 1:2], rs[2][:, 0:1], mv[2][:, 0:1], ALU.mult).then_inc(S["skip_ab_ready"], 1)
                o.end()
            elif name in ("K", "Q"):
                k = name.lower()
                o = Order(pool, f"pool{k}_order", 1 if k == "k" else 2, n)
                after(pool, f"{k}_sum", n + 1)
                apart(pool)
                o(pool.tensor_scalar(qk_ms[k][:, :], qk_sum[k][:, :], 1.0 / D, RMS_EPS, ALU.mult, ALU.add))
                root = pool.tensor_tensor(qk_r[k][:, :], qk_ms[k][:, :], minus_half[:, 0:1], ALU.pow)
                if k == "k":
                    root.then_inc(S["k_scale"], 1)
                else:
                    o(root)
                    apart(pool)
                    pool.tensor_scalar(q_neg[:, :], qk_r[k][:, :], -1.0, 1.0, ALU.mult, ALU.mult)\
                        .then_inc(S["q_scale"], 1)
                o.end()

        def whole(eng, item, fori):
            for name in ("res0", "T1", "res1", "AG1", "GT1", "LN1a", "TG1", "res2", "LN1b", "res3", "res4", "WB1",
                         "res5", "LN2b", "res6"):
                item(eng, name, -1, 0, -1, 1)
            for t in range(TPC):
                for name, ahead in START_STEPS if t < TPC - 1 else LAST_START_STEPS:
                    if t + ahead >= 0:
                        item(eng, name, -1, t + ahead, -1, 1)
                    if (name, t) == ("T1", 0):
                        item(eng, f"res{PIECES - 1}", -1, 0, -1, 1)
            if item is act_item or item is dve_item:
                for name in ("hi0", "hi1", "hi2", "lo0", "lo1", "lo2"):
                    item(eng, name, -1, TPC - 1, 0, 1)

            def chunk(c, par, **which):
                for name, f, t in chunk_items(**which):
                    item(eng, name, f, t, c, par)

            chunk(0, 0, with1=True, with3=False, first=True)
            chunk(1, 1, with1=True, with3=True)
            with fori(0, (NCH - 4) // 2) as pair:
                chunk(pair * 2 + 2, 0, with1=True, with3=True)
                chunk(pair * 2 + 3, 1, with1=True, with3=True)
            chunk(NCH - 2, 0, with1=True, with3=True)
            chunk(NCH - 1, 1, with1=False, with3=True)
            for name in TAIL_STEPS.split():
                item(eng, name, 0, STAGE3[name][1] - 3 if name in STAGE3 else 0, NCH, 0)

        block = ctx.enter_context(nc.Block())

        @block.sync
        def _(sp):
            sp.dma_start(x0[0][:, :], x[0:P, :]).then_inc(x_loaded[0], 16)
            sp.dma_start(const[:, :], consts).then_inc(S["const_loaded"], 16)
            sp.dma_start(half_bias[:, :], bias).then_inc(S["const_loaded"], 16)
            sp.dma_start(gbias[:, :], gate_bias).then_inc(S["const_loaded"], 16)
            sp_load_x(sp, 0, 0)
            for i in range(PIECES):
                if i == PIECES - 1:
                    sp_load_x(sp, 1, 1)
                after(sp, "res_hi_ready", i - 1)
                after(sp, "res_lo_ready", i - 1)
                sp.dma_start(raw[i % 2][:, 0:PIECE], resident[i]).then_inc(raw_loaded[i % 2], 16)
            for i in range(2):
                after(sp, "res_hi_ready", PIECES - 1 + i)
                after(sp, "res_lo_ready", PIECES - 1 + i)
                sp_load_record(sp, i, i)
            whole(sp, sp_item, sp.Fori)
            for t in range(TPC):
                sp.wait_ge(out_stored[t], 16 * NCH)

        @block.gpsimd
        def _(pool):
            pool.memset(minus_half[:, :], -0.5).then_inc(S["const_ready"], 1)
            pool.wait_ge(S["const_ready"], 1)
            pool.wait_ge(S["bias_ready"], 1)
            pool_rstd(pool, 1, 0)
            whole(pool, pool_item, pool.Fori)

        @block.scalar
        def _(act):
            whole(act, act_item, act.Fori)

        @block.vector
        def _(dve):
            dve.wait_ge(S["const_loaded"], 48)
            dve.tensor_scalar(half_bias[:, :], half_bias[:, :], 0.5, None, ALU.mult).then_inc(S["bias_ready"], 1)
            dve.wait_ge(x_loaded[0], 16)
            dve_stats(dve, 1, 0, x0[0][:, :])
            dve_norm(dve, 1, 0, x0[0][:, :])
            whole(dve, dve_item, dve.Fori)

        @block.tensor
        def _(pe):
            pe.wait_ge(S["const_loaded"], 48)
            whole(pe, pe_item, pe.Fori)


def kernel(L0_attn_x, L0_attn_w_qkv, L0_attn_w_swiglu, L0_attn_w_out, L0_ffn_W, L0_ffn_b, L0_ffn_lora_A,
           L0_ffn_lora_B, L0_ffn_gate_w, L0_ffn_gate_b):
    import concourse.bacc as bacc
    from concourse.bass_utils import run_bass_kernel_spmd

    def arr(a):
        return np.asarray(a)

    def by_k(w):
        o, i = w.shape
        return w.T.reshape(i // P, P, o).transpose(1, 0, 2).reshape(P, -1)

    xs = arr(L0_attn_x).reshape(TOKENS, D)
    ag = np.concatenate([arr(L0_ffn_lora_A).reshape(ER, D), arr(L0_ffn_gate_w)], 0)
    lora_b = arr(L0_ffn_lora_B).transpose(0, 2, 1).reshape(ER, D)
    wq, wk, wv = (arr(L0_attn_w_qkv)[i * D:(i + 1) * D] for i in range(3))
    resident = np.concatenate([by_k(ag), lora_b, by_k(arr(L0_ffn_W)), by_k(wk), by_k(wv), by_k(wq)], 1)
    resident = np.ascontiguousarray(resident.reshape(P, PIECES, PIECE).transpose(1, 0, 2))
    up, gate = arr(L0_attn_w_swiglu)[:DFF], arr(L0_attn_w_swiglu)[DFF:]
    w_out = arr(L0_attn_w_out).T
    stream = np.stack([
        np.concatenate([by_k(gate[f * P:(f + 1) * P]), by_k(up[f * P:(f + 1) * P]),
                        w_out[(f - 1) % NF * P:((f - 1) % NF + 1) * P]], 1) for f in range(NF)])
    arrays = {
        "x_rows": np.ascontiguousarray(np.concatenate([xs, xs[:P]], 0)),
        "resident": resident,
        "stream": np.ascontiguousarray(stream),
        "bias": np.ascontiguousarray(np.broadcast_to(arr(L0_ffn_b), (P, D))),
        "gate_bias": np.ascontiguousarray(np.broadcast_to(arr(L0_ffn_gate_b), (P, E))),
        "consts": np.concatenate([np.eye(P, dtype=np.float32), np.ones((P, P), np.float32),
                                  np.tile(np.arange(E, dtype=np.float32), (P, 1))], 1),
    }
    nc = bacc.Bacc("TRN2", target_bir_lowering=False, num_devices=1, dynamic_dma_scratch_size=8192)
    args = [nc.dram_tensor(name, a.shape, F32, kind="ExternalInput").ap() for name, a in arrays.items()]
    out = nc.dram_tensor("out_rows", (TOKENS, D), F32, kind="ExternalOutput").ap()
    build_program(nc, *args, out)
    got = run_bass_kernel_spmd(nc, [arrays], core_ids=[0]).results[0]["out_rows"]
    return got.reshape(L0_attn_x.shape)
```
